# Optimizing a Trainium2 kernel written in Bass

```python
import numpy as np
import jax
import jax.numpy as jnp

def _softmax(x, axis=-1):
    return jax.nn.softmax(x, axis=axis)

def _gelu(x):
    return jax.nn.gelu(x, approximate=True)

def _silu(x):
    return jax.nn.silu(x)

def _sigmoid(x):
    return jax.nn.sigmoid(x)

def _layernorm(x, axis=-1, eps=1e-05):
    m = jnp.mean(x, axis=axis, keepdims=True)
    v = jnp.var(x, axis=axis, keepdims=True)
    return (x - m) / jnp.sqrt(v + eps)

def _scatter_add(tgt, idx, src, axis=0):
    return tgt.at[idx].add(src)

def _segment_sum(src, seg, n):
    return jax.ops.segment_sum(src, seg, n)
kernel_name = 'mk_gnn_resnorm_d4_gnn_r32_dba441'

def setup_inputs(seed: int=0):
    np.random.seed(seed)
    _w = jnp.asarray

    def _rec_inputs():
        import jax
        import jax.numpy as jnp
        _gk = jax.random.key(seed)
        x = -0.0003713 + 1 * jax.random.normal(jax.random.fold_in(_gk, 1), (3125, 256), jnp.float32)
        _s = jax.random.randint(jax.random.fold_in(_gk, 2), (25000,), 0, 3125, jnp.int32)
        _d = jax.random.randint(jax.random.fold_in(_gk, 3), (25000,), 0, 3125, jnp.int32)
        _loop = jnp.arange(3125, dtype=jnp.int32)
        src = jnp.concatenate([_s, _d, _loop])
        dst = jnp.concatenate([_d, _s, _loop])
        _o = jnp.argsort(dst, stable=True)
        src = src[_o]
        dst = dst[_o]
        edge_attr_3 = -1.09012e-05 + 0.99985 * jax.random.normal(jax.random.fold_in(_gk, 12), (53125, 3), jnp.float32)
        return (x, src, dst, edge_attr_3)
    x, src, dst, edge_attr_3 = _rec_inputs()

    def _L0_gnn_setup():
        import jax, jax.numpy as jnp
        import numpy as np
        N = 50000
        E = 12500
        IN = 256
        H = 8
        D = 32
        EF = 3
        key = jax.random.key(seed)
        ks = jax.random.split(key, 8)
        x = jax.random.normal(ks[0], (N, IN), dtype=jnp.float32)
        edge_index = jax.random.randint(ks[1], (2, E), 0, N, dtype=jnp.int64)
        edge_attr = jax.random.normal(ks[2], (E, EF), dtype=jnp.float32)
        W = jax.random.normal(ks[3], (H * D, IN), dtype=jnp.float32) * np.float32(np.sqrt(2.0 / (IN + H * D)))
        a_src = jax.random.normal(ks[4], (H, D), dtype=jnp.float32) * np.float32(np.sqrt(2.0 / (H + D)))
        a_dst = jax.random.normal(ks[5], (H, D), dtype=jnp.float32) * np.float32(np.sqrt(2.0 / (H + D)))
        edge_W = jax.random.normal(ks[6], (H * D, EF), dtype=jnp.float32) * np.float32(np.sqrt(2.0 / (EF + H * D)))
        edge_b = jnp.zeros((H * D,), dtype=jnp.float32)
        bias = jnp.zeros((H * D,), dtype=jnp.float32)
        return {'x': x, 'W': W, 'a_src': a_src, 'a_dst': a_dst, 'edge_W': edge_W, 'edge_b': edge_b, 'bias': bias, 'edge_attr': edge_attr, 'edge_index': edge_index}
    _L0_gnn_all = _L0_gnn_setup()
    _L0_gnn_in = {k: v for k, v in _L0_gnn_all.items() if k in ('W', 'a_src', 'a_dst', 'edge_W', 'edge_b', 'bias')}
    del _L0_gnn_all

    def _L1_gnn_setup():
        import jax, jax.numpy as jnp
        import numpy as np
        N_NODES = 50000
        N_EDGES = 25000
        D_IN = 256
        D_HID = 256
        D_OUT = 256

        def _sage_conv(x, src, dst, Wl, bl, Wr, num_nodes):
            msg = x[src]
            agg = jax.ops.segment_sum(msg, dst, num_segments=num_nodes)
            deg = jax.ops.segment_sum(jnp.ones((src.shape[0],), x.dtype), dst, num_segments=num_nodes)
            mean = agg / jnp.maximum(deg, 1.0)[:, None]
            return jnp.einsum('nd,od->no', mean, Wl) + bl + jnp.einsum('nd,od->no', x, Wr)
        key = jax.random.key(seed)
        ks = jax.random.split(key, 12)
        x = jax.random.normal(ks[0], (N_NODES, D_IN), dtype=jnp.float32)
        edge_index = jax.random.randint(ks[1], (2, N_EDGES), 0, N_NODES, dtype=jnp.int32)

        def lin(k, dout, din):
            return jax.random.normal(k, (dout, din), dtype=jnp.float32) * (1.0 / np.sqrt(din))
        return {'x': x, 'edge_index': edge_index, 'W1l': lin(ks[2], D_HID, D_IN), 'b1l': jnp.zeros((D_HID,), jnp.float32), 'W1r': lin(ks[3], D_HID, D_IN), 'W2l': lin(ks[4], D_HID, D_HID), 'b2l': jnp.zeros((D_HID,), jnp.float32), 'W2r': lin(ks[5], D_HID, D_HID), 'W3l': lin(ks[6], D_OUT, D_HID), 'b3l': jnp.zeros((D_OUT,), jnp.float32), 'W3r': lin(ks[7], D_OUT, D_HID)}
    _L1_gnn_all = _L1_gnn_setup()
    _L1_gnn_in = {k: v for k, v in _L1_gnn_all.items() if k in ('W1l', 'b1l', 'W1r', 'W2l', 'b2l', 'W2r', 'W3l', 'b3l', 'W3r')}
    del _L1_gnn_all

    def _L2_gnn_setup():
        import jax, jax.numpy as jnp
        import numpy as np
        N_NODES = 50000
        N_EDGES = 25000
        D_IN = 256
        D_OUT = 256
        key = jax.random.key(seed)
        k1, k2, k3, k4 = jax.random.split(key, 4)
        x = jax.random.normal(k1, (N_NODES, D_IN), dtype=jnp.float32)
        edge_index = jax.random.randint(k2, (2, N_EDGES), 0, N_NODES, dtype=jnp.int64)
        glorot = (6.0 / (D_IN + D_OUT)) ** 0.5
        W = jax.random.uniform(k3, (D_OUT, D_IN), minval=-glorot, maxval=glorot, dtype=jnp.float32)
        b = jnp.zeros((D_OUT,), dtype=jnp.float32)
        return {'x': x, 'edge_index': edge_index, 'W': W, 'b': b}
    _L2_gnn_all = _L2_gnn_setup()
    _L2_gnn_in = {k: v for k, v in _L2_gnn_all.items() if k in ('W', 'b')}
    del _L2_gnn_all

    def _L3_gnn_setup():
        import jax, jax.numpy as jnp
        import numpy as np
        N_NODES = 10000
        N_EDGES = 10000
        FEA = 256
        HID = 256
        HEADS = 4
        ODIM = HID // HEADS
        NEG_SLOPE = 0.2

        def _gat_layer(x, W, al, ar, b, src, dst):
            n = x.shape[0]
            z = (x @ W).reshape(n, HEADS, ODIM)
            el = jnp.sum(z * al, axis=-1)
            er = jnp.sum(z * ar, axis=-1)
            e = jax.nn.leaky_relu(el[src] + er[dst], negative_slope=NEG_SLOPE)
            e_max = jax.ops.segment_max(e, dst, num_segments=n)
            ex = jnp.exp(e - e_max[dst])
            denom = jax.ops.segment_sum(ex, dst, num_segments=n)
            alpha = ex / denom[dst]
            msg = z[src] * alpha[:, :, None]
            out = jax.ops.segment_sum(msg, dst, num_segments=n)
            out = out + x.reshape(n, HEADS, ODIM)
            out = out + b.reshape(HEADS, ODIM)
            out = jax.nn.elu(out)
            return out.reshape(n, HID)
        key = jax.random.key(seed)
        ks = jax.random.split(key, 12)
        inp = {'features': jax.random.normal(ks[0], (N_NODES, FEA), dtype=jnp.float32), 'src': jax.random.randint(ks[1], (N_EDGES,), 0, N_NODES, dtype=jnp.int32), 'dst': jax.random.randint(ks[2], (N_EDGES,), 0, N_NODES, dtype=jnp.int32), 'W0': jax.random.normal(ks[3], (FEA, HID), dtype=jnp.float32) * (1.0 / np.sqrt(FEA)), 'al0': jax.random.normal(ks[4], (HEADS, ODIM), dtype=jnp.float32) * 0.1, 'ar0': jax.random.normal(ks[5], (HEADS, ODIM), dtype=jnp.float32) * 0.1, 'b0': jnp.zeros((HID,), dtype=jnp.float32), 'W1': jax.random.normal(ks[6], (HID, HID), dtype=jnp.float32) * (1.0 / np.sqrt(HID)), 'al1': jax.random.normal(ks[7], (HEADS, ODIM), dtype=jnp.float32) * 0.1, 'ar1': jax.random.normal(ks[8], (HEADS, ODIM), dtype=jnp.float32) * 0.1, 'b1': jnp.zeros((HID,), dtype=jnp.float32)}
        return inp
    _L3_gnn_all = _L3_gnn_setup()
    _L3_gnn_in = {k: v for k, v in _L3_gnn_all.items() if k in ('W0', 'al0', 'ar0', 'b0', 'W1', 'al1', 'ar1', 'b1')}
    del _L3_gnn_all
    return {'x': x, 'src': src, 'dst': dst, 'edge_attr_3': edge_attr_3, 'L0_gnn_W': _L0_gnn_in['W'], 'L0_gnn_a_src': _L0_gnn_in['a_src'], 'L0_gnn_a_dst': _L0_gnn_in['a_dst'], 'L0_gnn_edge_W': _L0_gnn_in['edge_W'], 'L0_gnn_edge_b': _L0_gnn_in['edge_b'], 'L0_gnn_bias': _L0_gnn_in['bias'], 'L1_gnn_W1l': _L1_gnn_in['W1l'], 'L1_gnn_b1l': _L1_gnn_in['b1l'], 'L1_gnn_W1r': _L1_gnn_in['W1r'], 'L1_gnn_W2l': _L1_gnn_in['W2l'], 'L1_gnn_b2l': _L1_gnn_in['b2l'], 'L1_gnn_W2r': _L1_gnn_in['W2r'], 'L1_gnn_W3l': _L1_gnn_in['W3l'], 'L1_gnn_b3l': _L1_gnn_in['b3l'], 'L1_gnn_W3r': _L1_gnn_in['W3r'], 'L2_gnn_W': _L2_gnn_in['W'], 'L2_gnn_b': _L2_gnn_in['b'], 'L3_gnn_W0': _L3_gnn_in['W0'], 'L3_gnn_al0': _L3_gnn_in['al0'], 'L3_gnn_ar0': _L3_gnn_in['ar0'], 'L3_gnn_b0': _L3_gnn_in['b0'], 'L3_gnn_W1': _L3_gnn_in['W1'], 'L3_gnn_al1': _L3_gnn_in['al1'], 'L3_gnn_ar1': _L3_gnn_in['ar1'], 'L3_gnn_b1': _L3_gnn_in['b1']}

def reference(x, src, dst, edge_attr_3, L0_gnn_W, L0_gnn_a_src, L0_gnn_a_dst, L0_gnn_edge_W, L0_gnn_edge_b, L0_gnn_bias, L1_gnn_W1l, L1_gnn_b1l, L1_gnn_W1r, L1_gnn_W2l, L1_gnn_b2l, L1_gnn_W2r, L1_gnn_W3l, L1_gnn_b3l, L1_gnn_W3r, L2_gnn_W, L2_gnn_b, L3_gnn_W0, L3_gnn_al0, L3_gnn_ar0, L3_gnn_b0, L3_gnn_W1, L3_gnn_al1, L3_gnn_ar1, L3_gnn_b1):
    import jax
    import jax.numpy as jnp

    def _L0_gnn_ref(x, W, a_src, a_dst, edge_W, edge_b, bias, edge_attr, edge_index):
        import jax, jax.numpy as jnp
        import numpy as np
        N = 50000
        E = 12500
        IN = 256
        H = 8
        D = 32
        EF = 3
        n = x.shape[0]
        h = (x @ W.T).reshape(n, H, D)
        src, dst = (edge_index[0], edge_index[1])
        h_src = h[src]
        h_dst = h[dst]
        alpha = jnp.einsum('ehd,hd->eh', h_src, a_src) + jnp.einsum('ehd,hd->eh', h_dst, a_dst)
        enc = jax.nn.relu(edge_attr @ edge_W.T + edge_b).reshape(-1, H, D)
        alpha = alpha + jnp.sum(enc * h_dst, axis=-1)
        alpha = jnp.where(alpha >= 0, alpha, 0.2 * alpha)
        amax = jax.ops.segment_max(alpha, dst, num_segments=n)
        ex = jnp.exp(alpha - amax[dst])
        denom = jax.ops.segment_sum(ex, dst, num_segments=n)
        attn = ex / jnp.maximum(denom[dst], 1e-10)
        out = jax.ops.segment_sum(h_src * attn[..., None], dst, num_segments=n)
        return out.reshape(n, H * D) + bias

    def _L1_gnn_ref(x, edge_index, W1l, b1l, W1r, W2l, b2l, W2r, W3l, b3l, W3r):
        import jax, jax.numpy as jnp
        import numpy as np
        N_NODES = 50000
        N_EDGES = 25000
        D_IN = 256
        D_HID = 256
        D_OUT = 256

        def _sage_conv(x, src, dst, Wl, bl, Wr, num_nodes):
            msg = x[src]
            agg = jax.ops.segment_sum(msg, dst, num_segments=num_nodes)
            deg = jax.ops.segment_sum(jnp.ones((src.shape[0],), x.dtype), dst, num_segments=num_nodes)
            mean = agg / jnp.maximum(deg, 1.0)[:, None]
            return jnp.einsum('nd,od->no', mean, Wl) + bl + jnp.einsum('nd,od->no', x, Wr)
        src, dst = (edge_index[0], edge_index[1])
        n = x.shape[0]
        h = _sage_conv(x, src, dst, W1l, b1l, W1r, n)
        h = jax.nn.relu(h)
        h = _sage_conv(h, src, dst, W2l, b2l, W2r, n)
        h = jax.nn.relu(h)
        h = _sage_conv(h, src, dst, W3l, b3l, W3r, n)
        return h

    def _L2_gnn_ref(x, edge_index, W, b):
        import jax, jax.numpy as jnp
        import numpy as np
        N_NODES = 50000
        N_EDGES = 25000
        D_IN = 256
        D_OUT = 256
        N = x.shape[0]
        loop = jnp.arange(N, dtype=edge_index.dtype)
        src = jnp.concatenate([edge_index[0], loop])
        dst = jnp.concatenate([edge_index[1], loop])
        deg = jax.ops.segment_sum(jnp.ones_like(src, dtype=x.dtype), dst, num_segments=N)
        deg_inv_sqrt = jnp.where(deg > 0, jax.lax.rsqrt(jnp.maximum(deg, 1.0)), 0.0)
        norm = deg_inv_sqrt[src] * deg_inv_sqrt[dst]
        h = jnp.einsum('nd,od->no', x, W)
        msg = h[src] * norm[:, None]
        out = jax.ops.segment_sum(msg, dst, num_segments=N) + b
        return jax.nn.relu(out)

    def _L3_gnn_ref(features, src, dst, W0, al0, ar0, b0, W1, al1, ar1, b1):
        import jax, jax.numpy as jnp
        import numpy as np
        N_NODES = 10000
        N_EDGES = 10000
        FEA = 256
        HID = 256
        HEADS = 4
        ODIM = HID // HEADS
        NEG_SLOPE = 0.2

        def _gat_layer(x, W, al, ar, b, src, dst):
            n = x.shape[0]
            z = (x @ W).reshape(n, HEADS, ODIM)
            el = jnp.sum(z * al, axis=-1)
            er = jnp.sum(z * ar, axis=-1)
            e = jax.nn.leaky_relu(el[src] + er[dst], negative_slope=NEG_SLOPE)
            e_max = jax.ops.segment_max(e, dst, num_segments=n)
            ex = jnp.exp(e - e_max[dst])
            denom = jax.ops.segment_sum(ex, dst, num_segments=n)
            alpha = ex / denom[dst]
            msg = z[src] * alpha[:, :, None]
            out = jax.ops.segment_sum(msg, dst, num_segments=n)
            out = out + x.reshape(n, HEADS, ODIM)
            out = out + b.reshape(HEADS, ODIM)
            out = jax.nn.elu(out)
            return out.reshape(n, HID)
        x = _gat_layer(features, W0, al0, ar0, b0, src, dst)
        x = _gat_layer(x, W1, al1, ar1, b1, src, dst)
        return x
    edge_index = jnp.stack([src, dst])
    x = _layernorm(x + _L0_gnn_ref(x, L0_gnn_W, L0_gnn_a_src, L0_gnn_a_dst, L0_gnn_edge_W, L0_gnn_edge_b, L0_gnn_bias, edge_attr_3, edge_index), axis=-1)
    x = _layernorm(x + _L1_gnn_ref(x, edge_index, L1_gnn_W1l, L1_gnn_b1l, L1_gnn_W1r, L1_gnn_W2l, L1_gnn_b2l, L1_gnn_W2r, L1_gnn_W3l, L1_gnn_b3l, L1_gnn_W3r), axis=-1)
    x = _layernorm(x + _L2_gnn_ref(x, edge_index, L2_gnn_W, L2_gnn_b), axis=-1)
    x = _layernorm(x + _L3_gnn_ref(x, src, dst, L3_gnn_W0, L3_gnn_al0, L3_gnn_ar0, L3_gnn_b0, L3_gnn_W1, L3_gnn_al1, L3_gnn_ar1, L3_gnn_b1), axis=-1)
    return x

_drawn_inputs = setup_inputs


def setup_inputs(seed=0):
    import zlib

    import numpy as np

    out = dict(_drawn_inputs(seed))
    spreads = {'L0_gnn_edge_b': (0.0, 0.1),
     'L0_gnn_bias': (0.0, 0.1),
     'L1_gnn_b1l': (0.0, 0.1),
     'L1_gnn_b2l': (0.0, 0.1),
     'L1_gnn_b3l': (0.0, 0.1),
     'L2_gnn_b': (0.0, 0.1),
     'L3_gnn_b0': (0.0, 0.1),
     'L3_gnn_b1': (0.0, 0.1)}
    factors = {'L3_gnn_ar0': 10.519, 'L3_gnn_ar1': 13.178}
    for name, (base, spread) in spreads.items():
        noise = np.random.default_rng([zlib.crc32(name.encode()), seed]).standard_normal(out[name].shape)
        drawn = base * np.exp(spread * noise) if base else spread * noise
        out[name] = jnp.asarray(drawn.astype(out[name].dtype))
    for name, factor in factors.items():
        out[name] = (out[name] * factor).astype(out[name].dtype)
    return out
```

```python
import concourse.bass as bass
from concourse import mybir
from contextlib import ExitStack


F32 = mybir.dt.float32
I32 = mybir.dt.int32
ALU = mybir.AluOpType
ACT = mybir.ActivationFunctionType
AX = mybir.AxisListType

N, E, D = 3125, 53125, 256
P = 128
FC = D // P
TILES = -(-E // P)
TILES += -TILES % 32
PAD_E = TILES * P
NPAD = -(-N // (5 * P)) * 5 * P
CH = 5 * P
NCH = NPAD // CH
SPLITS = [(0, 512), (512, CH - 512)]
WIDE = NPAD + P
BIG = 1.0e30
EPS = 1e-5
TW = D + 16

LAYERS = [("gat_edge", 8, 8, D + 16), ("sum", 16, 0, D), ("sum", 16, 0, D), ("sum", 16, 0, D),
          ("sum", 16, 0, D), ("gat", 16, 4, D + 8), ("gat", 16, 4, D + 8)]
NL = len(LAYERS)
GROUPS = [TILES // l[1] for l in LAYERS]
RING = 4
BANKS = 3
LAG = 2
ATT = [l for l in range(NL) if LAYERS[l][0] != "sum"]
LN_STAGES = [0, 3, 4, 6]
ROOT_STAGES = [0, 1, 2, 3]
DEN_STAGES = [0, 3, 5, 6]
FROM_ACT_STAGES = [3, 4, 5, 6]
LOADS = 22
LOADED = 16 * LOADS
ATT_GROUPS = [sum(GROUPS[m] for m in ATT if m < l) for l in range(NL)]
ALL_GROUPS = [sum(GROUPS[:l]) for l in range(NL)]
CONSTS = 3 + 3 * 9
HALF_TILES = 16 * TILES // 2
DST_BEFORE = {0: 0, 5: 2 * GROUPS[0], 6: 2 * GROUPS[0] + GROUPS[5]}
TABLE_SEM = [16 * NCH * (s + max(0, s - 5)) for s in range(NL + 1)]
SEG_BEFORE = {0: 0, 5: 24 * GROUPS[0], 6: 24 * GROUPS[0] + 16 * GROUPS[5]}


def gnn_program(nc, a, out, stop):
    last_stage = NL - 1 if stop is None else stop
    ctx = ExitStack()
    with ctx:
        def sb(name, shape, dt=F32):
            return ctx.enter_context(nc.sbuf_tensor(name, shape, dt))

        def sem(name):
            return ctx.enter_context(nc.semaphore(name))

        xT = sb("xT", [P, FC, NPAD])
        rT = sb("rT", [P, FC, NPAD])
        acc = sb("acc", [P, FC, WIDE])
        den = sb("den", [9, WIDE])
        norm = sb("norm", [P, NPAD])
        w_table = [sb(f"w_table{s}", [P, FC, TW if s in (0, 5, 6) else D]) for s in range(NL)]
        w_root = {s: sb(f"w_root{s}", [P, FC, D]) for s in (1, 2, 3)}
        bias = sb("bias", [P, 7, FC])
        w_edge = sb("w_edge", [4, D])
        ident = sb("ident", [P, P])
        iota_i = sb("iota_i", [P, P], I32)
        iota_f = sb("iota_f", [P, P])
        mean_w = sb("mean_w", [P, P])
        eps = sb("eps", [P, 1])
        one = sb("one", [1, 1])
        head_of = {8: sb("head_of8", [8, FC, P]), 4: sb("head_of4", [4, FC, P])}
        same_head = {8: sb("same_head8", [8, 8, 8]), 4: sb("same_head4", [4, 16, 4])}
        head_col = {8: sb("head_col8", [P, FC, 8]), 4: sb("head_col4", [P, FC, 4])}
        deg_row = sb("deg_row", [9, P])
        spread_f = {8: sb("spread_f8", [64, D]), 4: sb("spread_f4", [64, D])}
        spread_h = {8: sb("spread_h8", [64, 8]), 4: sb("spread_h4", [64, 4])}
        own_tile = {8: sb("own_tile8", [64, 8]), 4: sb("own_tile4", [64, 16])}
        src_idx = sb("src_idx", [P, TILES], I32)
        dst_idx = sb("dst_idx", [P, TILES], I32)
        base_all = sb("base_all", [P, TILES], I32)
        local = sb("local", [P, TILES])
        rows = sb("rows", [P, 2 * 16 * TW])
        drows = sb("drows", [P, 2, 4, TW])
        src_now = sb("src_now", [P, 2, 16], I32)
        dst_now = sb("dst_now", [P, 2, 16], I32)
        dsmall = sb("dsmall", [P, 2, 16, 4])
        onehot = sb("onehot", [P, RING, P])
        msg = sb("msg", [P, RING, D])
        attr = sb("attr", [4, 2, 8 * P])
        prod = sb("prod", [P, 4, D])
        al = sb("al", [P, 64])
        al2 = sb("al2", [P, 64])
        al3 = sb("al3", [P, 64])
        dseg = sb("dseg", [64, 2, P + 2], I32)
        dlast = sb("dlast", [1, 2, 8 * 17], I32)
        pen = sb("pen", [64, P + 1])
        pen_first = sb("pen_first", [64, P])
        pen_row = sb("pen_row", [1, 8 * 17])
        fwd = sb("fwd", [64, P])
        bwd = sb("bwd", [64, P])
        segmax = sb("segmax", [64, P])
        shifted = sb("shifted", [64, P])
        last_row = sb("last_row", [1, 8 * 17])
        carry_row = sb("carry_row", [1, 8 * 17])
        carry_th = sb("carry_th", [1, 64])
        rescale = sb("rescale", [64, 1])
        resc_f = [sb(f"resc_f{p}", [P, 32]) for p in range(2)]
        resc_h = [sb(f"resc_h{p}", [8, 16]) for p in range(2)]
        rescale_e = sb("rescale_e", [64, 1])
        rescale_t = sb("rescale_t", [64, 16])
        ex8 = sb("ex8", [P, 2, 8, 9])
        ex4 = sb("ex4", [P, 2, 16, 4])
        part = [rows[:, i * FC * CH:(i + 1) * FC * CH].rearrange("p (f n) -> p f n", f=FC) for i in range(5)]
        v, c, t = part[:3]
        st = part[3]
        st2 = part[4]
        tb = rows[:, 5 * FC * CH:5 * FC * CH + 5 * TW].rearrange("p (k w) -> p k w", k=5)

        ps = ctx.enter_context(nc.psum_tensor("ps", [P, 8, 512], F32))
        enc_ps = [ps[:, 0, 0:D], ps[:, 1, 0:D]]
        sum_ps = [ps[:, 2 + b, 0:D].rearrange("p (f n) -> p f n", f=FC) for b in range(BANKS)]
        den_ps = [ps[0:9, 2 + b, D:D + P] for b in range(BANKS)]
        alT_ps = ps[0:64, 5, 0:P]
        carry_ps = ps[0:64, 5, P:P + 1]
        last_ps = ps[0:1, 5, 192:256]
        back_ps = ps[:, 5, 256:320]
        resc_ps = ps[:, 5, 320:352]
        resch_ps = ps[0:8, 5, 352:368]
        ex_ps = [ps[:, 6 + p, 0:64] for p in range(2)]

        def wide(b):
            return ps[:, b:b + 2, :].rearrange("p b n -> p (b n)")

        tables = [nc.dram_tensor(f"table{l}", (NPAD, LAYERS[l][3]), F32, kind="Internal").ap() for l in range(NL)]
        scores = {l: nc.dram_tensor(f"scores{l}", (NPAD, 4), F32, kind="Internal").ap() for l in (5, 6)}

        loaded = sem("loaded")
        consts = sem("consts")
        built = sem("built")
        src_landed = [sem("src_landed0"), sem("src_landed1")]
        dst_landed = [sem("dst_landed0"), sem("dst_landed1")]
        rows_free = sem("rows_free")
        drows_free = sem("drows_free")
        seg_landed = [sem("seg_landed0"), sem("seg_landed1")]
        seg_free = sem("seg_free")
        enc_ready = sem("enc_ready")
        enc_free = sem("enc_free")
        tile_ready = sem("tile_ready")
        sum_ready = sem("sum_ready")
        added = sem("added")
        rescaled = sem("rescaled")
        al_ready = sem("al_ready")
        alT_ready = sem("alT_ready")
        scans_ready = sem("scans_ready")
        last_ready = sem("last_ready")
        carry_ready = sem("carry_ready")
        carryT_ready = sem("carryT_ready")
        shift_ready = sem("shift_ready")
        back_ready = sem("back_ready")
        ex_ready = sem("ex_ready")
        rexp_ready = sem("rexp_ready")
        resct_ready = sem("resct_ready")
        resc_ready = sem("resc_ready")
        resc_copied = sem("resc_copied")
        dve_step = sem("dve_step")
        act_step = sem("act_step")
        den_bc = sem("den_bc")
        v_ready = sem("v_ready")
        mean_ready = sem("mean_ready")
        c_ready = sem("c_ready")
        sq_ready = sem("sq_ready")
        var_ready = sem("var_ready")
        std_ready = sem("std_ready")
        to_act = sem("to_act")
        from_act = sem("from_act")
        st_ready = sem("st_ready")
        root_ready = sem("root_ready")
        root_out = sem("root_out")
        row_ready = sem("row_ready")
        row_out = sem("row_out")
        table_written = sem("table_written")
        tb_free = sem("tb_free")
        passed = sem("passed")
        built_pe = sem("built_pe")
        pool_step = sem("pool_step")
        out_written = sem("out_written")

        class Steps:

            def __init__(self, eng, s):
                self.eng, self.s, self.base, self.k, self.i, self.per = eng, s, 0, 0, 0, 0

            def enter(self, i, per):
                self.i, self.per, self.k = i, per, 0

            def leave(self, turns):
                assert self.k == self.per, (self.k, self.per)
                self.base += turns * self.per
                self.i, self.per, self.k = 0, 0, 0

            def done(self, ins):
                self.k += 1
                ins.then_inc(self.s, 1)
                return self.base + self.i * self.per + self.k

            def wait(self, at):
                self.eng.wait_ge(self.s, at)

            def then(self, ins):
                self.wait(self.done(ins))

            def flat(self):
                self.base += self.k
                self.k = 0

        n_edge_layers = last_stage + 1

        def wait_alone(eng, s, value):
            eng.wait_ge(s, value)
            eng.sem_inc(passed, 1)

        def group_loop(eng, l, step, tail):
            ng = GROUPS[l]
            step((0, 0), 0, True)
            with eng.Fori(0, ng // 2 - 1) as i:
                step((2 * i + 1, i), 1, False)
                step((2 * i + 2, i + 1), 0, False)
            step((ng - 1, (ng - 1) // 2), 1, False)
            tail((ng, ng // 2), 0)

        def store_tables(sp, s):
            last = s == last_stage
            with sp.Fori(0, NCH) as i:
                sp.wait_ge(row_out, 5 * NCH * (s + 1) + 5 * i + 5)
                if last:
                    sp.dma_start(out[bass.ds(i * CH, CH), :].rearrange("(k p) w -> p k w", p=P),
                                 tb[:, :, 0:D]).then_inc(out_written, 16)
                    sp.wait_ge(out_written, 16 * i + 16)
                    sp.sem_inc(tb_free, 1)
                else:
                    w = LAYERS[s + 1][3]
                    sp.dma_start(tables[s + 1][bass.ds(i * CH, CH), :].rearrange("(k p) w -> p k w", p=P),
                                 tb[:, :, 0:w]).then_inc(table_written, 16)
                    if s + 1 in scores:
                        sp.dma_start(scores[s + 1][bass.ds(i * CH, CH), :].rearrange("(k p) w -> p k w", p=P),
                                     tb[:, :, D + 4:D + 8]).then_inc(table_written, 16)
                    sp.wait_ge(table_written, TABLE_SEM[s + 1] + (TABLE_SEM[s + 2] - TABLE_SEM[s + 1]) // NCH * (i + 1))
                    sp.sem_inc(tb_free, 1)

        def src_rows(l, par):
            T, W = LAYERS[l][1], LAYERS[l][3]
            return rows[:, par * 16 * TW:par * 16 * TW + T * W].rearrange("p (t w) -> p t w", t=T)

        def edge_pe(pe, l):
            kind, T, H, W = LAYERS[l]
            mm = nc.tensor.matmul
            tb0 = TILES * l
            pe.wait_ge(row_out, 5 * NCH * (l + 1))

            def sums(g, par, k):
                r = k % RING
                bank = banks[k]
                lhs = src_rows(l, par)[:, k, 0:D] if kind == "sum" else msg[:, r, :]
                pe.wait_ge(tile_ready, tb0 + g[0] * T + k + 1)
                for f in range(FC):
                    ins = mm(sum_ps[bank][:, f, :], lhs[:, f * P:(f + 1) * P], onehot[:, r, :], start=True, stop=True)
                if kind == "gat_edge":
                    ins = mm(den_ps[bank], ex8[:, par, k, :], onehot[:, r, :], start=True, stop=True)
                elif kind == "gat":
                    ins = mm(den_ps[bank][0:4, :], ex4[:, par, k, :], onehot[:, r, :], start=True, stop=True)
                ins.then_inc(sum_ready, 1)

            banks = [k % BANKS for k in range(T)]
            if kind == "sum":
                def step(g, par, _first):
                    pe.wait_ge(src_landed[par], HALF_TILES * l + (g[1] + 1) * 16 * T)
                    for k in range(T):
                        sums(g, par, k)
                group_loop(pe, l, step, lambda g, p: None)
                return

            ag = ATT_GROUPS[l]

            def step(g, par, first):
                prev = (g[0] - 1, None)
                quarter = T // 4

                def prev_sums(q):
                    if not first:
                        for k in range(q * quarter, (q + 1) * quarter):
                            sums(prev, 1 - par, k)

                n = ag + g[0] + 1
                if kind == "gat_edge":
                    pe.wait_ge(seg_landed[par], 48 * (g[1] + 1))
                    for k in range(T):
                        pe.wait_ge(enc_free, g[0] * T + k + 1)
                        mm(enc_ps[k % 2], attr[:, par, k * P:(k + 1) * P], w_edge[:, :],
                           start=True, stop=True).then_inc(enc_ready, 1)
                if not (first and l == 0):
                    pe.wait_ge(resc_copied, n - 1)
                wait_alone(pe, al_ready, n)
                nc.tensor.transpose(alT_ps, al3[:, :], ident[:, :]).then_inc(alT_ready, 1)
                prev_sums(0)
                wait_alone(pe, scans_ready, n)
                mm(last_ps, fwd[:, P - 1:P], ident[0:64, 0:64], start=True, stop=True).then_inc(last_ready, 1)
                prev_sums(1)
                wait_alone(pe, carry_ready, n)
                mm(carry_ps, carry_th[:, :], one[:, :], start=True, stop=True).then_inc(carryT_ready, 1)
                prev_sums(2)
                wait_alone(pe, shift_ready, n)
                nc.tensor.transpose(back_ps, shifted[:, :], ident[0:64, 0:64]).then_inc(back_ready, 1)
                prev_sums(3)
                pe.wait_ge(ex_ready, n)
                wait_alone(pe, resct_ready, n)
                for f in range(FC):
                    mm(resc_ps[:, f * T:(f + 1) * T], spread_f[H][:, f * P:(f + 1) * P],
                       rescale_t[:, 0:T], start=True, stop=True)
                mm(resch_ps[0:H, 0:T], spread_h[H][:, :], rescale_t[:, 0:T], start=True, stop=True).then_inc(resc_ready, 1)

            def tail(g, par):
                for k in range(T):
                    sums((g[0] - 1, None), 1, k)

            group_loop(pe, l, step, tail)

        def node_pe(pe, s):
            mm = nc.tensor.matmul
            cb = NCH * (s + 1)
            last = s == last_stage
            if s >= 0:
                pe.wait_ge(added, TILES * (s + 1) + 1)
            with pe.Fori(0, NCH) as i:
                if s >= 0:
                    pe.wait_ge(row_out, 5 * cb + 5 * i)
                if s in ATT:
                    H = LAYERS[s][2]
                    for lo, n in SPLITS:
                        for f in range(FC):
                            ins = mm(wide(2 * f)[:, lo:lo + n], head_of[H][:, f, :], den[0:H, bass.ds(i * CH + lo, n)],
                                     start=True, stop=True)
                if s in (0, 3):
                    for lo, n in SPLITS:
                        ins = mm(wide(4)[:, lo:lo + n], deg_row[:, :], den[0:9, bass.ds(i * CH + lo, n)],
                                 start=True, stop=True)
                if s in DEN_STAGES:
                    ins.then_inc(den_bc, 1)
                if s in LN_STAGES:
                    lb = NCH * LN_STAGES.index(s)
                    for src, ready, done, b in ((v, v_ready, mean_ready, 0), (t, sq_ready, var_ready, 2)):
                        pe.wait_ge(ready, lb + i + 1)
                        for lo, n in SPLITS:
                            for f in range(FC):
                                ins = mm(wide(b)[:, lo:lo + n], mean_w[:, :], src[:, f, lo:lo + n],
                                         start=f == 0, stop=f == 1)
                        ins.then_inc(done, 1)
                pe.wait_ge(st_ready, cb + i + 1)
                x = st2 if s == 3 else st
                if s in ROOT_STAGES and not last:
                    rb = NCH * ROOT_STAGES.index(s)
                    w = w_root[s + 1] if s < 3 else w_table[4]
                    for f in range(FC):
                        for lo, n in SPLITS:
                            for k in range(FC):
                                ins = mm(wide(4 + 2 * f)[:, lo:lo + n], w[:, k, f * P:(f + 1) * P],
                                         x[:, k, lo:lo + n], start=k == 0, stop=k == 1)
                    ins.then_inc(root_ready, 1)
                for k in range(5):
                    b = k % 4
                    if k == 4:
                        pe.wait_ge(row_out, 5 * cb + 5 * i + 1)
                    if last:
                        for f in range(FC):
                            ins = nc.tensor.transpose(ps[:, b, f * P:(f + 1) * P], st[:, f, k * P:(k + 1) * P], ident[:, :])
                    else:
                        w = LAYERS[s + 1][3]
                        for f in range(FC):
                            ins = mm(ps[:, b, 0:w], x[:, f, k * P:(k + 1) * P], w_table[s + 1][:, f, 0:w],
                                     start=f == 0, stop=f == 1)
                    ins.then_inc(row_ready, 1)

        def edge_act(act, l):
            H = LAYERS[l][2]

            def step(g, par, first):
                n = ATT_GROUPS[l] + g[0] + 1
                act.wait_ge(shift_ready, n)
                nc.scalar.activation(rescale_e[:, :], rescale[:, :], ACT.Exp).then_inc(rexp_ready, 1)
                act.wait_ge(back_ready, n)
                ex = (ex8 if H == 8 else ex4)[:, par, :, 0:H]
                nc.scalar.activation(ex, back_ps.rearrange("p (t h) -> p t h", h=H), ACT.Exp)
                nc.scalar.activation(ex_ps[par], back_ps, ACT.Exp).then_inc(ex_ready, 1)
                act.wait_ge(resc_ready, n)
                T = LAYERS[l][1]
                nc.scalar.activation(resc_f[par][:, 0:FC * T], resc_ps[:, 0:FC * T], ACT.Copy)
                nc.scalar.activation(resc_h[par][0:H, 0:T], resch_ps[0:H, 0:T], ACT.Copy).then_inc(resc_copied, 1)

            group_loop(act, l, step, lambda g, p: None)

        def node_act(act, s):
            cb = NCH * (s + 1)
            last = s == last_stage
            with act.Fori(0, NCH) as i:
                cols = bass.ds(i * CH, CH)
                if s == -1:
                    nc.scalar.activation(st[:, :, :], xT[:, :, cols], ACT.Copy).then_inc(st_ready, 1)
                if s > 0:
                    act.wait_ge(to_act, NCH * (s - 1) + i + 1)
                if s == 3:
                    nc.scalar.activation(c[:, 1, :], c[:, 0, :], ACT.Sqrt).then_inc(from_act, 1)
                if s in (1, 2):
                    nc.scalar.activation(st[:, :, :], v[:, :, :], ACT.Relu).then_inc(st_ready, 1)
                if s == 4:
                    for f in range(FC):
                        ins = nc.scalar.activation(t[:, f, :], v[:, f, :], ACT.Relu, bias=bias[:, 4, f:f + 1])
                    ins.then_inc(from_act, 1)
                if s in (5, 6):
                    nc.scalar.activation(t[:, :, :], c[:, :, :], ACT.Exp).then_inc(from_act, 1)
                if s in LN_STAGES:
                    lb = NCH * LN_STAGES.index(s)
                    act.wait_ge(c_ready, lb + i + 1)
                    nc.scalar.activation(t[:, :, :], c[:, :, :], ACT.Square).then_inc(sq_ready, 1)
                    act.wait_ge(var_ready, lb + i + 1)
                    nc.scalar.activation(v[:, 0, :], wide(2)[:, 0:CH], ACT.Sqrt, bias=eps[:, :]).then_inc(std_ready, 1)
                if s in (0, 3, 4, 5) and not last:
                    act.wait_ge(st_ready, cb + i + 1)
                    nc.scalar.activation((rT if s == 5 else xT)[:, :, cols], st[:, :, :], ACT.Copy)
                if s in ROOT_STAGES and not last:
                    act.wait_ge(root_ready, NCH * ROOT_STAGES.index(s) + i + 1)
                    for f in range(FC):
                        if s < 3:
                            ins = nc.scalar.activation(rT[:, f, cols], wide(4 + 2 * f)[:, 0:CH], ACT.Identity,
                                                       bias=bias[:, s + 1, f:f + 1])
                        else:
                            ins = nc.scalar.activation(acc[:, f, cols], wide(4 + 2 * f)[:, 0:CH], ACT.Copy)
                w = D if last else LAYERS[s + 1][3]
                act.wait_ge(tb_free, cb + i + 1)
                for k in range(5):
                    act.wait_ge(row_ready, 5 * cb + 5 * i + k + 1)
                    nc.scalar.activation(tb[:, k, 0:w], ps[:, k % 4, 0:w], ACT.Copy).then_inc(row_out, 1)

        def edge_dve(dve, l, ch):
            V = nc.vector
            kind, T, H, W = LAYERS[l]
            tb0 = TILES * l
            ag = ATT_GROUPS[l]

            def make_onehot(g, k):
                return V.tensor_scalar(onehot[:, k % RING, :], iota_f[:, :], local[:, bass.ds(g[0] * T + k, 1)],
                                       None, ALU.is_equal)

            def add_sums(g, par, k):
                now = tb0 + g[0] * T + k
                dve.wait_ge(sum_ready, now + 1)
                dve.wait_ge(added, now + 1)
                base = V.value_load(base_all[0:1, bass.ds(g[0] * T + k, 1)], min_val=0, max_val=N)
                if kind != "sum":
                    col = acc[:, :, bass.ds(base, 1)]
                    scale = resc_f[par][:, 0:FC * T].rearrange("p (f t) -> p f t", f=FC)[:, :, k:k + 1]
                    V.tensor_tensor(col, col, scale, ALU.mult)
                    dcol = den[0:H, bass.ds(base, 1)]
                    V.tensor_tensor(dcol, dcol, resc_h[par][0:H, k:k + 1], ALU.mult).then_inc(rescaled, 1)
                    dve.wait_ge(rescaled, TILES * ATT.index(l) + g[0] * T + k + 1)
                    nd = 9 if H == 8 else H
                    dwin = den[0:nd, bass.ds(base, P)]
                    V.tensor_tensor(dwin, dwin, den_ps[k % BANKS][0:nd, :], ALU.add)
                win = acc[:, :, bass.ds(base, P)]
                V.tensor_tensor(win, win, sum_ps[k % BANKS], ALU.add).then_inc(added, 1)

            if kind == "sum":
                def step(g, par, first):
                    for k in range(T + LAG):
                        if k < T:
                            make_onehot(g, k).then_inc(tile_ready, 1)
                        if k >= LAG:
                            add_sums(g, par, k - LAG)
                    dve.sem_inc(rows_free, 1)

                group_loop(dve, l, step, lambda g, p: None)
                return

            grid = lambda x: x[:, :].rearrange("p (t h) -> p t h", h=H)
            row = lambda x: x[0:1, 0:H * (T + 1)].rearrange("o (h t) -> o h t", h=H)

            def messages(g, par, q):
                src = src_rows(l, par)
                if q == 0:
                    dve.wait_ge(ex_ready, ag + g[0] + 1)
                    dve.wait_ge(resc_copied, ag + g[0] + 1)
                for k in range(q * T // 4, (q + 1) * T // 4 + (LAG if q == 3 else 0)):
                    if k < T:
                        make_onehot(g, k)
                        V.tensor_tensor(msg[:, k % RING, :].rearrange("p (h d) -> p h d", h=H),
                                        src[:, k, 0:D].rearrange("p (h d) -> p h d", h=H),
                                        ex_ps[par][:, k * H:(k + 1) * H].unsqueeze(2).broadcast_to([P, H, D // H]),
                                        ALU.mult).then_inc(tile_ready, 1)
                    if k >= LAG:
                        add_sums(g, par, k - LAG)
                if q == 3:
                    dve.sem_inc(rows_free, 1)

            def step(g, par, first):
                n = ag + g[0] + 1
                src = src_rows(l, par)
                prev = (g[0] - 1, None)

                def prev_messages(q):
                    if not first:
                        messages(prev, 1 - par, q)

                dve.wait_ge(seg_landed[par], SEG_BEFORE[l] + (48 if H == 8 else 32) * (g[1] + 1))
                V.tensor_tensor(pen[:, :], dseg[:, par, 1:P + 2], dseg[:, par, 0:P + 1], ALU.not_equal)
                V.tensor_scalar(pen_first[:, :], dseg[:, par, 1:P + 1], dseg[:, par, 0:1], -BIG, ALU.not_equal, ALU.mult)
                marks = row(dlast[:, par, :])
                ch.then(V.tensor_tensor(row(pen_row)[:, :, 1:], marks[:, :, 1:], marks[:, :, 0:T], ALU.not_equal))
                V.tensor_scalar(row(pen_row)[:, :, 1:], row(pen_row)[:, :, 1:], -BIG, None, ALU.mult)
                ch.then(V.tensor_scalar(pen[:, :], pen[:, :], -BIG, None, ALU.mult))
                if kind == "gat_edge":
                    for hf in range(2):
                        dve.wait_ge(dst_landed[hf], 64 * (g[0] + 1))
                        at = None
                        for k in range(4 * hf, 4 * hf + 5):
                            if k < 4 * hf + 4:
                                dve.wait_ge(enc_ready, g[0] * T + k + 1)
                                now = ch.done(V.scalar_tensor_tensor(prod[:, k % 4, :], enc_ps[k % 2], 0.0,
                                                                     drows[:, hf, k % 4, 0:D], ALU.max, ALU.mult))
                            if at is not None:
                                ch.wait(at)
                                dve.sem_inc(enc_free, 1)
                                last = V.tensor_reduce(grid(al)[:, k - 1, :],
                                                       prod[:, (k - 1) % 4, :].rearrange("p (h d) -> p h d", h=H), AX.X, ALU.add)
                            at = now
                        ch.then(last)
                        ch.then(V.tensor_tensor(grid(al2)[:, 4 * hf:4 * hf + 4, :], grid(al)[:, 4 * hf:4 * hf + 4, :],
                                                drows[:, hf, :, D + 8:D + 16], ALU.add))
                        dve.sem_inc(drows_free, 1)
                    dve.wait_ge(src_landed[par], HALF_TILES * l + (g[1] + 1) * 16 * T)
                    ch.then(V.tensor_tensor(grid(al), grid(al2), src[:, :, D:D + 8], ALU.add))
                else:
                    dve.wait_ge(dst_landed[par], HALF_TILES * ATT.index(l) + (g[1] + 1) * 16 * T)
                    dve.wait_ge(src_landed[par], HALF_TILES * l + (g[1] + 1) * 16 * T)
                    ch.then(V.tensor_tensor(grid(al), dsmall[:, par, :, :], src[:, :, D:D + 4], ALU.add))
                    dve.sem_inc(drows_free, 1)
                dve.sem_inc(seg_free, 1)
                V.scalar_tensor_tensor(al3[:, :], al[:, :], 0.2, al[:, :], ALU.mult, ALU.max).then_inc(al_ready, 1)
                prev_messages(0)
                dve.wait_ge(alT_ready, n)
                V.tensor_tensor_scan(fwd[:, :], pen[:, 0:P], alT_ps, -BIG, ALU.add, ALU.max)
                V.tensor_tensor_scan(bwd[:, ::-1], pen[:, 1:P + 1][:, ::-1], alT_ps[:, ::-1], -BIG, ALU.add,
                                     ALU.max).then_inc(scans_ready, 1)
                dve.wait_ge(scans_ready, n)
                V.tensor_tensor(segmax[:, :], fwd[:, :], bwd[:, :], ALU.max)
                prev_messages(1)
                dve.wait_ge(last_ready, n)
                ch.then(V.tensor_copy(row(last_row)[:, :, 1:], last_ps.rearrange("o (t h) -> o h t", h=H)))
                ch.then(V.tensor_tensor_scan(carry_row[0:1, 0:H * (T + 1)], pen_row[0:1, 0:H * (T + 1)],
                                             last_row[0:1, 0:H * (T + 1)], -BIG, ALU.add, ALU.max))
                V.tensor_copy(row(last_row)[:, :, 0:1], row(carry_row)[:, :, T:T + 1])
                V.tensor_copy(carry_th[:, :].rearrange("o (t h) -> o h t", h=H),
                              row(carry_row)[:, :, 0:T]).then_inc(carry_ready, 1)
                prev_messages(2)
                dve.wait_ge(carryT_ready, n)
                ch.then(V.scalar_tensor_tensor(segmax[:, :], pen_first[:, :], carry_ps, segmax[:, :], ALU.add, ALU.max))
                V.tensor_tensor(shifted[:, :], alT_ps, segmax[:, :], ALU.subtract)
                V.tensor_scalar(rescale[:, :], carry_ps, segmax[:, 0:1], 0.0, ALU.subtract, ALU.min).then_inc(shift_ready, 1)
                prev_messages(3)
                dve.wait_ge(rexp_ready, n)
                V.tensor_scalar(rescale_t[:, 0:T], own_tile[H][:, :], rescale_e[:, 0:1], None, ALU.mult).then_inc(resct_ready, 1)

            def tail(g, par):
                for q in range(4):
                    messages((g[0] - 1, None), 1, q)

            V.memset(last_row[:, :], -BIG)
            ch.then(V.memset(pen_row[:, :], -BIG))
            ng = GROUPS[l]
            step((0, 0), 0, True)
            ch.flat()
            with dve.Fori(0, ng // 2 - 1) as i:
                ch.enter(i, 2 * CHAIN_STEPS[kind])
                step((2 * i + 1, i), 1, False)
                step((2 * i + 2, i + 1), 0, False)
                ch.leave(ng // 2 - 1)
            step((ng - 1, (ng - 1) // 2), 1, False)
            tail((ng, ng // 2), 0)
            ch.flat()

        def node_dve(dve, s, ch):
            V = nc.vector
            cb = NCH * (s + 1)
            last = s == last_stage
            dve.wait_ge(added, TILES * (s + 1) + 1)
            both = lambda x: x.unsqueeze(1).broadcast_to([P, FC, CH])
            with dve.Fori(0, NCH) as i:
                ch.enter(i, NODE_STEPS[s])
                cols = bass.ds(i * CH, CH)
                dve.wait_ge(st_ready, cb + i)
                if s in ATT:
                    dve.wait_ge(den_bc, NCH * DEN_STAGES.index(s) + i + 1)
                    ch.then(V.tensor_scalar(t[:, :, :], ps[:, 0:4, :].rearrange("p (f b) n -> p f (b n)", f=FC)[:, :, 0:CH],
                                            1e-10 if s == 0 else 1e-30, None, ALU.max))
                    ch.then(V.reciprocal(t[:, :, :], t[:, :, :]))
                    ch.then(V.tensor_tensor(v[:, :, :], acc[:, :, cols], t[:, :, :], ALU.mult))
                    for f in range(FC):
                        ins = V.scalar_tensor_tensor(v[:, f, :], v[:, f, :], bias[:, s, f:f + 1],
                                                     (rT if s == 6 else xT)[:, f, cols], ALU.add, ALU.add)
                    if s == 0:
                        ch.then(V.tensor_scalar(c[:, 1, :], wide(4)[:, 0:CH], 1.0, None, ALU.max))
                        V.reciprocal(norm[:, cols], c[:, 1, :]).then_inc(v_ready, 1)
                    else:
                        ch.then(ins)
                        V.tensor_scalar(c[:, :, :], v[:, :, :], 0.0, None, ALU.min).then_inc(to_act, 1)
                        dve.wait_ge(from_act, NCH * FROM_ACT_STAGES.index(s) + i + 1)
                        if s == 5:
                            dve.wait_ge(row_out, 5 * cb + 5 * i)
                            V.scalar_tensor_tensor(st[:, :, :], t[:, :, :], -1.0, v[:, :, :], ALU.add, ALU.max).then_inc(st_ready, 1)
                        else:
                            ch.then(V.scalar_tensor_tensor(v[:, :, :], t[:, :, :], -1.0, v[:, :, :], ALU.add, ALU.max))
                            V.tensor_tensor(v[:, :, :], v[:, :, :], xT[:, :, cols], ALU.add).then_inc(v_ready, 1)
                elif s == 4:
                    V.tensor_tensor(v[:, :, :], acc[:, :, cols], both(norm[:, cols]), ALU.mult).then_inc(to_act, 1)
                    dve.wait_ge(from_act, NCH * FROM_ACT_STAGES.index(s) + i + 1)
                    V.tensor_tensor(v[:, :, :], t[:, :, :], xT[:, :, cols], ALU.add).then_inc(v_ready, 1)
                else:
                    if s == 3:
                        dve.wait_ge(den_bc, NCH * DEN_STAGES.index(s) + i + 1)
                        V.tensor_scalar(c[:, 0, :], wide(4)[:, 0:CH], 1.0, None, ALU.add).then_inc(to_act, 1)
                    ch.then(V.tensor_tensor(v[:, :, :], acc[:, :, cols], both(norm[:, cols]), ALU.mult))
                    ins = V.tensor_tensor(v[:, :, :], v[:, :, :], rT[:, :, cols], ALU.add)
                    if s < 3:
                        ins.then_inc(to_act, 1)
                        dve.wait_ge(st_ready, cb + i + 1)
                    else:
                        ch.then(ins)
                        V.tensor_tensor(v[:, :, :], v[:, :, :], xT[:, :, cols], ALU.add).then_inc(v_ready, 1)
                        wait_alone(dve, from_act, i + 1)
                        norm_at = ch.done(V.reciprocal(norm[:, cols], c[:, 1, :]))
                if s in LN_STAGES:
                    lb = NCH * LN_STAGES.index(s)
                    dve.wait_ge(mean_ready, lb + i + 1)
                    if s == 3:
                        ch.wait(norm_at)
                    V.tensor_tensor(c[:, :, :], v[:, :, :], both(wide(0)[:, 0:CH]), ALU.subtract).then_inc(c_ready, 1)
                    dve.wait_ge(std_ready, lb + i + 1)
                    ch.then(V.reciprocal(v[:, 1, :], v[:, 0, :]))
                    dve.wait_ge(row_out, 5 * cb + 5 * i)
                    ins = V.tensor_tensor(st[:, :, :], c[:, :, :], both(v[:, 1, :]), ALU.mult)
                    if s == 3:
                        ch.then(ins)
                        ins = V.tensor_tensor(st2[:, :, :], st[:, :, :], both(norm[:, cols]), ALU.mult)
                    ins.then_inc(st_ready, 1)
                ch.leave(NCH)
            if not last:
                if s != 3:
                    V.memset(acc[:, :, :], 0.0)
                if s + 1 in ATT:
                    V.memset(den[:, :], 0.0)

        block = ctx.enter_context(nc.Block())

        @block.sync
        def _(sp):
            n_loads = [0]

            def load(dst, src):
                n_loads[0] += 1
                sp.dma_start(dst, src).then_inc(loaded, 16)

            load(xT[:, :, :], a["xT"].rearrange("(f p) n -> p f n", p=P))
            load(src_idx[:, :], a["src_idx"])
            load(dst_idx[:, :], a["dst_idx"])
            load(base_all[:, :], a["base_row"].partition_broadcast(P))
            load(bias[:, :, :], a["biases"].rearrange("p (l f) -> p l f", f=FC))
            for s in range(NL):
                load(w_table[s][:, :, 0:D], a[f"w_table{s}"].rearrange("(k p) o -> p k o", p=P))
            for s in w_root:
                load(w_root[s][:, :, :], a[f"w_root{s}"].rearrange("(k p) o -> p k o", p=P))
            load(w_edge[:, :], a["w_edge"])
            for n, s in enumerate((0, 5, 6)):
                load(part[n][:, :, 0:D], a[f"w_out{s}"].rearrange("(k p) i -> p k i", p=P))
                load(part[n][:, 0, D:D + 4], a[f"score_cols{s}"])
            assert n_loads[0] * 16 == LOADED, n_loads

            for l in ATT:
                if l >= n_edge_layers:
                    break
                kind, T, H, _ = LAYERS[l]

                def seg(g, par, _first, l=l, kind=kind, T=T, H=H):
                    sp.wait_ge(seg_free, ATT_GROUPS[l] + g[0] + 1)
                    sp.dma_start(dseg[:, par, :], a[f"dst_seg{H}"][bass.ds(64 * g[0], 64), :]).then_inc(seg_landed[par], 16)
                    sp.dma_start(dlast[0:1, par, 0:H * (T + 1)],
                                 a[f"dst_last{H}"][bass.ds(g[0], 1), :]).then_inc(seg_landed[par], 16)
                    if kind == "gat_edge":
                        sp.dma_start(attr[:, par, :], a["attrT"][:, bass.ds(T * P * g[0], T * P)]).then_inc(seg_landed[par], 16)

                if l == 0:
                    store_tables(sp, -1)
                    group_loop(sp, l, seg, lambda g, p: None)
                    for s in range(0, min(4, last_stage) + 1):
                        store_tables(sp, s)
                else:
                    group_loop(sp, l, seg, lambda g, p: None)
                    store_tables(sp, l)

        @block.gpsimd
        def _(pool):
            one_left = Steps(pool, consts)
            one_left.then(nc.gpsimd.memset(ident[:, :], 0.0))
            one_left.then(nc.gpsimd.affine_select(out=ident[:, :], in_=ident[:, :], compare_op=ALU.not_equal, fill=1.0,
                                                  base=0, pattern=[[-1, P]], channel_multiplier=1))
            one_left.then(nc.gpsimd.iota(iota_i[:, :], pattern=[[1, P]], base=0, channel_multiplier=0))

            def band(x, pattern, base, mult, width, base2=None):
                one_left.then(nc.gpsimd.memset(x, 1.0))
                one_left.then(nc.gpsimd.affine_select(out=x, in_=x, compare_op=ALU.is_ge, fill=0.0,
                                                      base=base, pattern=pattern, channel_multiplier=mult))
                one_left.then(nc.gpsimd.affine_select(out=x, in_=x, compare_op=ALU.is_ge, fill=0.0, base=width - 1 - base,
                                                      pattern=[[-s, n] for s, n in pattern], channel_multiplier=-mult))

            for H, T in ((8, 8), (4, 16)):
                band(head_of[H][:, :, :], [[P, FC], [1, P]], 0, -(D // H), D // H)
                band(same_head[H][:, :, :], [[0, T], [1, H]], 0, -1, 1)
                band(own_tile[H][:, :], [[-H, T]], 0, 1, H)
                band(head_col[H][:, :, :], [[P, FC], [-(D // H), H]], 0, 1, D // H)
            band(deg_row[:, :], [[0, P]], -8, 1, 1)
            assert one_left.k == CONSTS
            pool.sem_inc(rows_free, 2)
            pool.sem_inc(drows_free, 2)
            pool.sem_inc(seg_free, 2)
            pool.sem_inc(enc_free, 2)
            pool.sem_inc(tb_free, 1)
            pool.wait_ge(loaded, LOADED)
            ring = Steps(pool, pool_step)
            for l in range(n_edge_layers):
                kind, T, H, W = LAYERS[l]
                pool.wait_ge(table_written, TABLE_SEM[l + 1])

                def gather(g, par, _first, l=l, kind=kind, T=T, W=W):
                    pool.wait_ge(rows_free, ALL_GROUPS[l] + g[0] + 1)
                    at = ring.done(nc.gpsimd.tensor_copy(src_now[:, par, 0:T], src_idx[:, bass.ds(g[0] * T, T)]))
                    if kind != "sum":
                        at = ring.done(nc.gpsimd.tensor_copy(dst_now[:, par, 0:T], dst_idx[:, bass.ds(g[0] * T, T)]))
                    wait_alone(pool, pool_step, at)
                    if kind == "gat":
                        wait_alone(pool, drows_free, DST_BEFORE[l] + g[0] + 1)
                    for k in range(T):
                        if kind == "gat_edge":
                            if k % 4 == 0:
                                wait_alone(pool, drows_free, 2 * g[0] + k // 4 + 1)
                            pool.indirect_dma_start(
                                drows[:, k // 4, k % 4, :], None, tables[l][:, :],
                                bass.IndirectOffsetOnAxis(ap=dst_now[:, par, k:k + 1], axis=0)).then_inc(dst_landed[k // 4], 16)
                        elif kind == "gat":
                            pool.indirect_dma_start(
                                dsmall[:, par, k, :], None, scores[l][:, :],
                                bass.IndirectOffsetOnAxis(ap=dst_now[:, par, k:k + 1], axis=0)).then_inc(dst_landed[par], 16)
                        pool.indirect_dma_start(
                            src_rows(l, par)[:, k, :], None, tables[l][:, :],
                            bass.IndirectOffsetOnAxis(ap=src_now[:, par, k:k + 1], axis=0)).then_inc(src_landed[par], 16)

                per = 2 if kind != "sum" else 1
                gather((0, 0), 0, True)
                ring.flat()
                with pool.Fori(0, GROUPS[l] // 2 - 1) as i:
                    ring.enter(i, 2 * per)
                    gather((2 * i + 1, i), 1, False)
                    gather((2 * i + 2, i + 1), 0, False)
                    ring.leave(GROUPS[l] // 2 - 1)
                gather((GROUPS[l] - 1, GROUPS[l] // 2 - 1), 1, False)
                ring.flat()

        @block.tensor
        def _(pe):
            mm = nc.tensor.matmul
            pe.wait_ge(loaded, LOADED)
            pe.wait_ge(consts, CONSTS)
            pe.wait_ge(built, 1)
            for n, (s, cols) in enumerate(((0, 16), (5, 8), (6, 8))):
                for m in range(FC):
                    for k in range(FC):
                        ins = mm(ps[:, 3 * m + n, 0:cols], part[n][:, k, m * P:(m + 1) * P],
                                 st[:, k, n * 16:n * 16 + cols], start=k == 0, stop=k == 1)
            ins.then_inc(built_pe, 1)
            for H, T in ((8, 8), (4, 16)):
                sh = same_head[H][:, :, :].rearrange("h t g -> h (t g)")
                mm(ps[0:64, 6, 0:D], sh, head_of[H][:, :, :].rearrange("h f p -> h (f p)"), start=True, stop=True)
                mm(ps[0:64, 7, 0:H], sh, ident[0:H, 0:H], start=True, stop=True).then_inc(built_pe, 1)
                pe.wait_ge(built, 2 if H == 8 else 3)
            node_pe(pe, -1)
            for l in range(n_edge_layers):
                edge_pe(pe, l)
                node_pe(pe, l)

        @block.scalar
        def _(act):
            act.wait_ge(loaded, LOADED)
            act.wait_ge(built, 3)
            node_act(act, -1)
            for l in range(n_edge_layers):
                if LAYERS[l][0] != "sum":
                    edge_act(act, l)
                node_act(act, l)

        @block.vector
        def _(dve):
            V = nc.vector
            ch = Steps(dve, dve_step)
            dve.sem_inc(added, 1)
            V.memset(mean_w[:, :], 1.0 / D)
            V.memset(eps[:, :], EPS)
            V.memset(one[:, :], 1.0)
            V.memset(ex8[:, :, :, 8:9], 1.0)
            V.memset(den[:, :], 0.0)
            V.memset(acc[:, :, :], 0.0)
            V.memset(st[:, :, 0:48], 0.0)
            dve.wait_ge(loaded, LOADED)
            dve.wait_ge(consts, CONSTS)
            V.tensor_copy(iota_f[:, :], iota_i[:, :])
            ch.then(V.tensor_tensor(local[:, :], dst_idx[:, :], base_all[:, :], ALU.subtract))
            for n, H in enumerate((8, 4, 4)):
                for j in range(2):
                    for k in range(FC):
                        ins = V.tensor_scalar(st[:, k, 16 * n + j * H:16 * n + (j + 1) * H], head_col[H][:, k, :],
                                              part[n][:, 0, D + 2 * j + k:D + 2 * j + k + 1], None, ALU.mult)
            ins.then_inc(built, 1)
            dve.wait_ge(built_pe, 1)
            for n, (s, cols) in enumerate(((0, 16), (5, 8), (6, 8))):
                for m in range(FC):
                    V.tensor_copy(w_table[s][:, m, D:D + cols], ps[:, 3 * m + n, 0:cols])
            for n, H in enumerate((8, 4)):
                dve.wait_ge(built_pe, n + 2)
                V.tensor_copy(spread_f[H][:, :], ps[0:64, 6, 0:D])
                V.tensor_copy(spread_h[H][:, :], ps[0:64, 7, 0:H]).then_inc(built, 1)
            ch.flat()
            for l in range(n_edge_layers):
                dve.wait_ge(row_out, 5 * NCH * (l + 1))
                edge_dve(dve, l, ch)
                node_dve(dve, l, ch)


CHAIN_STEPS = {"gat_edge": 18, "gat": 6}
NODE_STEPS = {0: 5, 1: 1, 2: 1, 3: 5, 4: 1, 5: 4, 6: 6}

INS = (["xT", "src_idx", "dst_idx", "base_row", "biases", "w_edge", "attrT"] + [f"w_table{s}" for s in range(NL)]
       + ["w_root1", "w_root2", "w_root3"] + [f"{n}{s}" for s in (0, 5, 6) for n in ("w_out", "score_cols")]
       + ["dst_seg8", "dst_seg4", "dst_last8", "dst_last4"])


def lay_out(x, src, dst, edge_attr_3, **w):
    import numpy as np
    x, src, dst = np.asarray(x), np.asarray(src), np.asarray(dst)
    o = {}
    o["xT"] = np.zeros((D, NPAD), x.dtype)
    o["xT"][:, :N] = x.T
    dst_p = np.concatenate([np.full(1, -1, dst.dtype), dst, np.full(PAD_E - E + 1, N, dst.dtype)])
    src_p = np.concatenate([src, np.zeros(PAD_E - E, src.dtype)])
    o["src_idx"] = src_p.reshape(TILES, P).T
    o["dst_idx"] = dst_p[1:-1].reshape(TILES, P).T
    o["base_row"] = dst_p[1:-1:P]
    seg = np.stack([dst_p[t * P:t * P + P + 2] for t in range(TILES)])
    last = dst_p[0::P][:TILES + 1]
    for H, T in ((8, 8), (4, 16)):
        o[f"dst_seg{H}"] = np.repeat(seg, H, axis=0)
        o[f"dst_last{H}"] = np.stack([np.tile(last[g * T:g * T + T + 1], H) for g in range(TILES // T)])
    attr = np.asarray(edge_attr_3)
    o["attrT"] = np.zeros((4, PAD_E), attr.dtype)
    o["attrT"][:3, :E] = attr.T
    o["attrT"][3] = 1
    A = {k: np.asarray(z) for k, z in w.items()}
    o["w_edge"] = np.concatenate([A["L0_gnn_edge_W"].T, A["L0_gnn_edge_b"][None]])
    b = [A["L0_gnn_bias"], A["L1_gnn_b1l"], A["L1_gnn_b2l"], A["L1_gnn_b3l"], A["L2_gnn_b"], A["L3_gnn_b0"], A["L3_gnn_b1"]]
    o["biases"] = np.stack(b).reshape(7 * FC, P).T
    names = ["L0_gnn_W", "L1_gnn_W1l", "L1_gnn_W2l", "L1_gnn_W3l", "L2_gnn_W"]
    for s, n in enumerate(names):
        o[f"w_table{s}"] = A[n].T
    for s, n in ((1, "W1r"), (2, "W2r"), (3, "W3r")):
        o[f"w_root{s}"] = A["L1_gnn_" + n].T
    o["w_table5"], o["w_table6"] = A["L3_gnn_W0"], A["L3_gnn_W1"]
    o["w_out0"], o["w_out5"], o["w_out6"] = A["L0_gnn_W"], A["L3_gnn_W0"].T, A["L3_gnn_W1"].T
    for s, p, q in ((0, "L0_gnn_a_src", "L0_gnn_a_dst"), (5, "L3_gnn_al0", "L3_gnn_ar0"), (6, "L3_gnn_al1", "L3_gnn_ar1")):
        o[f"score_cols{s}"] = np.concatenate([A[p].reshape(FC, P), A[q].reshape(FC, P)]).T
    return o


STOP = None


def kernel(**inputs):
    import numpy as np
    import concourse.bacc as bacc
    from concourse.bass_utils import run_bass_kernel_spmd

    nc = bacc.Bacc("TRN2", target_bir_lowering=False, num_devices=1)
    o = lay_out(**inputs)
    arrays, args = {}, {}
    for name in INS:
        arr = np.ascontiguousarray(o[name])
        arrays[f"in_{name}"] = arr
        args[name] = nc.dram_tensor(f"in_{name}", arr.shape, mybir.dt.from_np(arr.dtype), kind="ExternalInput").ap()
    out = nc.dram_tensor("out_x", (NPAD, D), F32, kind="ExternalOutput").ap()
    gnn_program(nc, args, out, STOP)
    r = run_bass_kernel_spmd(nc, [arrays], core_ids=[0])
    return r.results[0]["out_x"][:N]
```

```python
import concourse.bass as bass
from concourse import mybir
from contextlib import ExitStack


F32 = mybir.dt.float32
I32 = mybir.dt.int32
ALU = mybir.AluOpType
ACT = mybir.ActivationFunctionType
AX = mybir.AxisListType

N, E, D = 3125, 53125, 256
P = 128
FC = D // P
TILES = -(-E // P)
TILES += -TILES % 32
PAD_E = TILES * P
NPAD = -(-N // (5 * P)) * 5 * P
CH = 5 * P
NCH = NPAD // CH
SPLITS = [(0, 512), (512, CH - 512)]
WIDE = NPAD + P
BIG = 1.0e30
EPS = 1e-5
TW = D + 16

T = 8
NG = TILES // T
SLOTS = T + 1
LAYERS = [("gat_edge", 8, D + 16), ("sum", 0, D), ("sum", 0, D), ("sum", 0, D), ("sum", 0, D),
          ("gat", 4, D + 8), ("gat", 4, D + 8)]
NL = len(LAYERS)
ATT = [l for l in range(NL) if LAYERS[l][0] != "sum"]
LN_STAGES = [0, 3, 4, 6]
ROOT_STAGES = [0, 1, 2, 3]
DEN_STAGES = [0, 3, 5, 6]
FROM_ACT_STAGES = [3, 4, 5, 6]
LOADS = 23
LOADED = 16 * LOADS
CONSTS = 3 + 3 * 5
HALF_TILES = 16 * TILES // 2
DST_BEFORE = {0: 0, 5: 2 * NG, 6: 3 * NG}
TABLE_SEM = [16 * NCH * (s + max(0, s - 5)) for s in range(NL + 1)]
SEG_BEFORE = {0: 0, 5: 24 * NG, 6: 40 * NG}


def gnn_program(nc, a, out, stop):
    last_stage = NL - 1 if stop is None else stop
    ctx = ExitStack()
    with ctx:
        def sb(name, shape, dt=F32):
            return ctx.enter_context(nc.sbuf_tensor(name, shape, dt))

        def sem(name):
            return ctx.enter_context(nc.semaphore(name))

        xT = sb("xT", [P, FC, NPAD])
        rT = sb("rT", [P, FC, NPAD])
        acc = sb("acc", [P, FC, WIDE])
        den = sb("den", [9, WIDE])
        norm = sb("norm", [P, NPAD])
        w_table = [sb(f"w_table{s}", [P, FC, TW if s in (0, 5, 6) else D]) for s in range(NL)]
        w_root = {s: sb(f"w_root{s}", [P, FC, D]) for s in (1, 2, 3)}
        bias = sb("bias", [P, 7, FC])
        w_edge = sb("w_edge", [4, D])
        ident = sb("ident", [P, P])
        iota = sb("iota", [P, T * P])
        mean_w = sb("mean_w", [P, P])
        eps = sb("eps", [P, 1])
        one = sb("one", [1, 1])
        head_of = {8: sb("head_of8", [8, FC, P]), 4: sb("head_of4", [4, FC, P])}
        head_col = {8: sb("head_col8", [P, FC, 8]), 4: sb("head_col4", [P, FC, 4])}
        deg_row = sb("deg_row", [9, P])
        src_idx = sb("src_idx", [P, TILES], I32)
        dst_idx = sb("dst_idx", [P, TILES], I32)
        base = sb("base", [P, NG], I32)
        last = sb("last", [1, NG], I32)
        windows = sb("windows", [1, NG], I32)
        local = sb("local", [P, TILES])
        rows = sb("rows", [P, 4 * T * TW])
        onehot = rows[:, 2 * T * TW:2 * T * TW + T * P].rearrange("p (t n) -> p t n", t=T)
        prod = rows[:, 2 * T * TW + T * P:2 * T * TW + T * P + 4 * D].rearrange("p (t d) -> p t d", t=4)
        msg = rows[:, 4 * T * TW - T * D:4 * T * TW].rearrange("p (t d) -> p t d", t=T)
        drows = sb("drows", [P, 2, 4, TW])
        src_now = sb("src_now", [P, 2, T], I32)
        dst_now = sb("dst_now", [P, 2, T], I32)
        dsmall = sb("dsmall", [P, 2, T, 4])
        attr = sb("attr", [4, 2, T * P])
        al = sb("al", [P, 64])
        al2 = sb("al2", [P, 64])
        al3 = sb("al3", [P, 64])
        dseg = sb("dseg", [64, 2, P + 2], I32)
        marks = sb("marks", [1, 2, 2 * 8 * SLOTS], I32)
        pen = sb("pen", [64, P + 1])
        pen_first = sb("pen_first", [64, P])
        pen_last = sb("pen_last", [64, P])
        pen_row = sb("pen_row", [1, 2 * 8 * SLOTS])
        fwd = sb("fwd", [64, P])
        bwd = sb("bwd", [64, P])
        segmax = sb("segmax", [64, P])
        shifted = sb("shifted", [64, P])
        edge_row = sb("edge_row", [1, 2 * 8 * SLOTS])
        carry_row = sb("carry_row", [1, 2 * 8 * SLOTS])
        carry_th = sb("carry_th", [1, 2, 64])
        rescale = sb("rescale", [8, 1])
        rescale_e = sb("rescale_e", [8, 1])
        resc_f = [sb(f"resc_f{p}", [P, FC]) for p in range(2)]
        resc_h = [sb(f"resc_h{p}", [8, 1]) for p in range(2)]
        ex8 = sb("ex8", [P, 2, T, 9])
        ex4 = sb("ex4", [P, 2, T, 4])
        part = [rows[:, i * FC * CH:(i + 1) * FC * CH].rearrange("p (f n) -> p f n", f=FC) for i in range(5)]
        v, c, t = part[:3]
        st = part[3]
        st2 = part[4]
        tb = rows[:, 5 * FC * CH:5 * FC * CH + 5 * TW].rearrange("p (k w) -> p k w", k=5)

        ps = ctx.enter_context(nc.psum_tensor("ps", [P, 8, 512], F32))
        enc_ps = [ps[:, 0, 0:D], ps[:, 1, 0:D]]
        sum_ps = [ps[:, 2 + f, 0:P] for f in range(FC)]
        sums_ps = ps[:, 2:4, 0:P]
        den_ps = ps[0:9, 4, 0:P]
        alT_ps = ps[0:64, 5, 0:P]
        carry_ps = ps[0:64, 5, P:P + 2]
        edge_ps = ps[0:1, 5, 192:320]
        back_ps = ps[:, 5, 320:384]
        resc_ps = ps[:, 5, 384:384 + FC]
        resch_ps = ps[0:8, 5, 388:389]
        ex_ps = [ps[:, 6 + p, 0:64] for p in range(2)]

        def wide(b):
            return ps[:, b:b + 2, :].rearrange("p b n -> p (b n)")

        tables = [nc.dram_tensor(f"table{l}", (NPAD, LAYERS[l][2]), F32, kind="Internal").ap() for l in range(NL)]
        scores = {l: nc.dram_tensor(f"scores{l}", (NPAD, 4), F32, kind="Internal").ap() for l in (5, 6)}

        loaded = sem("loaded")
        consts = sem("consts")
        built = sem("built")
        src_landed = [sem("src_landed0"), sem("src_landed1")]
        dst_landed = [sem("dst_landed0"), sem("dst_landed1")]
        rows_free = sem("rows_free")
        drows_free = sem("drows_free")
        seg_landed = [sem("seg_landed0"), sem("seg_landed1")]
        seg_free = sem("seg_free")
        enc_ready = sem("enc_ready")
        enc_free = sem("enc_free")
        tile_ready = sem("tile_ready")
        sum_ready = sem("sum_ready")
        added = sem("added")
        more_ready = sem("more_ready")
        more_summed = sem("more_summed")
        more_added = sem("more_added")
        rescaled = sem("rescaled")
        al_ready = sem("al_ready")
        alT_ready = sem("alT_ready")
        scans_ready = sem("scans_ready")
        last_ready = sem("last_ready")
        carry_ready = sem("carry_ready")
        carryT_ready = sem("carryT_ready")
        shift_ready = sem("shift_ready")
        back_ready = sem("back_ready")
        ex_ready = sem("ex_ready")
        resc_ready = sem("resc_ready")
        resc_copied = sem("resc_copied")
        dve_step = sem("dve_step")
        act_step = sem("act_step")
        den_bc = sem("den_bc")
        v_ready = sem("v_ready")
        mean_ready = sem("mean_ready")
        c_ready = sem("c_ready")
        sq_ready = sem("sq_ready")
        var_ready = sem("var_ready")
        std_ready = sem("std_ready")
        to_act = sem("to_act")
        from_act = sem("from_act")
        st_ready = sem("st_ready")
        root_ready = sem("root_ready")
        root_out = sem("root_out")
        row_ready = sem("row_ready")
        row_out = sem("row_out")
        table_written = sem("table_written")
        tb_free = sem("tb_free")
        passed = sem("passed")
        built_pe = sem("built_pe")
        pool_step = sem("pool_step")
        out_written = sem("out_written")

        class Steps:

            def __init__(self, eng, s):
                self.eng, self.s, self.base, self.k, self.i, self.per = eng, s, 0, 0, 0, 0

            def enter(self, i, per):
                self.i, self.per, self.k = i, per, 0

            def leave(self, turns):
                assert self.k == self.per, (self.k, self.per)
                self.base += turns * self.per
                self.i, self.per, self.k = 0, 0, 0

            def done(self, ins):
                self.k += 1
                ins.then_inc(self.s, 1)
                return self.base + self.i * self.per + self.k

            def wait(self, at):
                self.eng.wait_ge(self.s, at)

            def then(self, ins):
                self.wait(self.done(ins))

            def flat(self):
                self.base += self.k
                self.k = 0

        n_edge_layers = last_stage + 1

        def wait_alone(eng, s, value):
            eng.wait_ge(s, value)
            eng.sem_inc(passed, 1)

        def group_loop(eng, step, done=lambda: None, per=None, chain=None):
            step(0, 0, 0, True)
            if chain:
                chain.flat()
            with eng.Fori(0, NG // 2 - 1) as i:
                if chain:
                    chain.enter(i, 2 * per)
                step(2 * i + 1, i, 1, False)
                step(2 * i + 2, i + 1, 0, False)
                if chain:
                    chain.leave(NG // 2 - 1)
            step(NG - 1, NG // 2 - 1, 1, False)
            if chain:
                chain.flat()

        class Turns:

            def __init__(self, eng, name):
                self.eng, self.reg = eng, eng.alloc_register(name)
                eng.reg_mov(self.reg, 0)

            def now(self):
                return self.eng.snap(self.reg, min_val=0, max_val=NL * (NG + N // P + 1))

            def next(self):
                self.eng.reg_add(self.reg, self.reg, 1)

        def further_windows(eng, g, body):
            n = eng.value_load(windows[0:1, bass.ds(g, 1)], min_val=1, max_val=T)
            with eng.If(n > 1):
                with eng.Fori(1, n) as w:
                    body(w)
            eng.end_ifs()

        def store_tables(sp, s):
            last = s == last_stage
            with sp.Fori(0, NCH) as i:
                sp.wait_ge(row_out, 5 * NCH * (s + 1) + 5 * i + 5)
                if last:
                    sp.dma_start(out[bass.ds(i * CH, CH), :].rearrange("(k p) w -> p k w", p=P),
                                 tb[:, :, 0:D]).then_inc(out_written, 16)
                    sp.wait_ge(out_written, 16 * i + 16)
                    sp.sem_inc(tb_free, 1)
                else:
                    w = LAYERS[s + 1][2]
                    sp.dma_start(tables[s + 1][bass.ds(i * CH, CH), :].rearrange("(k p) w -> p k w", p=P),
                                 tb[:, :, 0:w]).then_inc(table_written, 16)
                    if s + 1 in scores:
                        sp.dma_start(scores[s + 1][bass.ds(i * CH, CH), :].rearrange("(k p) w -> p k w", p=P),
                                     tb[:, :, D + 4:D + 8]).then_inc(table_written, 16)
                    sp.wait_ge(table_written, TABLE_SEM[s + 1] + (TABLE_SEM[s + 2] - TABLE_SEM[s + 1]) // NCH * (i + 1))
                    sp.sem_inc(tb_free, 1)

        def src_rows(l, par):
            W = LAYERS[l][2]
            return rows[:, par * T * TW:par * T * TW + T * W].rearrange("p (t w) -> p t w", t=T)

        def edge_pe(pe, l, turns):
            kind, H, W = LAYERS[l]
            mm = nc.tensor.matmul
            TH = T * H
            pe.wait_ge(row_out, 5 * NCH * (l + 1))

            def tile_sums(par, k):
                lhs = src_rows(l, par)[:, k, 0:D] if kind == "sum" else msg[:, k, :]
                for f in range(FC):
                    ins = mm(sum_ps[f], lhs[:, f * P:(f + 1) * P], onehot[:, k, :], start=k == 0, stop=k == T - 1)
                if kind != "sum":
                    ex = (ex8 if H == 8 else ex4)[:, par, k, :]
                    ins = mm(den_ps[0:ex.shape[-1], :], ex, onehot[:, k, :], start=k == 0, stop=k == T - 1)
                return ins

            def sums(g, par, k):
                pe.wait_ge(tile_ready, TILES * l + g * T + k + 1)
                ins = tile_sums(par, k)
                if k == T - 1:
                    ins.then_inc(sum_ready, 1)

                    def window(w):
                        pe.wait_ge(more_ready, turns.now() + 1)
                        for kk in range(T):
                            more = tile_sums(par, kk)
                        more.then_inc(more_summed, 1)
                        turns.next()
                    further_windows(pe, g, window)

            if kind == "sum":
                def step(g, h, par, _first):
                    pe.wait_ge(src_landed[par], HALF_TILES * l + (h + 1) * 16 * T)
                    for k in range(T):
                        sums(g, par, k)
                group_loop(pe, step)
                return

            ag = NG * ATT.index(l)

            def step(g, h, par, first):
                def prev_sums(q):
                    if not first:
                        sums(g - 1, 1 - par, 2 * q)
                        sums(g - 1, 1 - par, 2 * q + 1)

                n = ag + g + 1
                if kind == "gat_edge":
                    pe.wait_ge(seg_landed[par], 48 * (h + 1))
                    for k in range(T):
                        pe.wait_ge(enc_free, g * T + k + 1)
                        mm(enc_ps[k % 2], attr[:, par, k * P:(k + 1) * P], w_edge[:, :],
                           start=True, stop=True).then_inc(enc_ready, 1)
                if not (first and l == 0):
                    pe.wait_ge(resc_copied, n - 1)
                wait_alone(pe, al_ready, n)
                nc.tensor.transpose(alT_ps[0:TH, :], al3[:, 0:TH], ident[:, :]).then_inc(alT_ready, 1)
                prev_sums(0)
                wait_alone(pe, scans_ready, n)
                mm(edge_ps[:, 0:TH], fwd[0:TH, P - 1:P], ident[0:TH, 0:TH], start=True, stop=True)
                mm(edge_ps[:, TH:2 * TH], bwd[0:TH, 0:1], ident[0:TH, 0:TH], start=True, stop=True).then_inc(last_ready, 1)
                prev_sums(1)
                wait_alone(pe, carry_ready, n)
                for j in range(2):
                    ins = mm(carry_ps[0:TH, j:j + 1], carry_th[:, j, 0:TH], one[:, :], start=True, stop=True)
                ins.then_inc(carryT_ready, 1)
                prev_sums(2)
                wait_alone(pe, shift_ready, n)
                nc.tensor.transpose(back_ps[:, 0:TH], shifted[0:TH, :], ident[0:TH, 0:TH]).then_inc(back_ready, 1)
                prev_sums(3)
                wait_alone(pe, ex_ready, n)
                for f in range(FC):
                    mm(resc_ps[:, f:f + 1], head_of[H][:, f, :], rescale_e[0:H, :], start=True, stop=True)
                mm(resch_ps[0:H, :], ident[0:H, 0:H], rescale_e[0:H, :], start=True, stop=True).then_inc(resc_ready, 1)

            group_loop(pe, step)
            for k in range(T):
                sums(NG - 1, 1, k)

        def node_pe(pe, s):
            mm = nc.tensor.matmul
            cb = NCH * (s + 1)
            last = s == last_stage
            if s >= 0:
                pe.wait_ge(added, NG * (s + 1) + 1)
                pe.wait_ge(rows_free, NG * (s + 1) + 2)
            with pe.Fori(0, NCH) as i:
                if s >= 0:
                    pe.wait_ge(row_out, 5 * cb + 5 * i)
                if s in ATT:
                    H = LAYERS[s][1]
                    for lo, n in SPLITS:
                        for f in range(FC):
                            ins = mm(wide(2 * f)[:, lo:lo + n], head_of[H][:, f, :], den[0:H, bass.ds(i * CH + lo, n)],
                                     start=True, stop=True)
                if s in (0, 3):
                    for lo, n in SPLITS:
                        ins = mm(wide(4)[:, lo:lo + n], deg_row[:, :], den[0:9, bass.ds(i * CH + lo, n)],
                                 start=True, stop=True)
                if s in DEN_STAGES:
                    ins.then_inc(den_bc, 1)
                if s in LN_STAGES:
                    lb = NCH * LN_STAGES.index(s)
                    for src, ready, done, b in ((v, v_ready, mean_ready, 0), (t, sq_ready, var_ready, 2)):
                        pe.wait_ge(ready, lb + i + 1)
                        for lo, n in SPLITS:
                            for f in range(FC):
                                ins = mm(wide(b)[:, lo:lo + n], mean_w[:, :], src[:, f, lo:lo + n],
                                         start=f == 0, stop=f == 1)
                        ins.then_inc(done, 1)
                pe.wait_ge(st_ready, cb + i + 1)
                x = st2 if s == 3 else st
                if s in ROOT_STAGES and not last:
                    rb = NCH * ROOT_STAGES.index(s)
                    w = w_root[s + 1] if s < 3 else w_table[4]
                    for f in range(FC):
                        for lo, n in SPLITS:
                            for k in range(FC):
                                ins = mm(wide(4 + 2 * f)[:, lo:lo + n], w[:, k, f * P:(f + 1) * P],
                                         x[:, k, lo:lo + n], start=k == 0, stop=k == 1)
                    ins.then_inc(root_ready, 1)
                for k in range(5):
                    b = k % 4
                    if k == 4:
                        pe.wait_ge(row_out, 5 * cb + 5 * i + 1)
                    if last:
                        for f in range(FC):
                            ins = nc.tensor.transpose(ps[:, b, f * P:(f + 1) * P], st[:, f, k * P:(k + 1) * P], ident[:, :])
                    else:
                        w = LAYERS[s + 1][2]
                        for f in range(FC):
                            ins = mm(ps[:, b, 0:w], x[:, f, k * P:(k + 1) * P], w_table[s + 1][:, f, 0:w],
                                     start=f == 0, stop=f == 1)
                    ins.then_inc(row_ready, 1)

        def edge_act(act, l):
            H = LAYERS[l][1]
            TH = T * H

            def step(g, h, par, first):
                n = NG * ATT.index(l) + g + 1
                act.wait_ge(shift_ready, n)
                nc.scalar.activation(rescale_e[0:H, :], rescale[0:H, :], ACT.Exp)
                act.wait_ge(back_ready, n)
                nc.scalar.activation((ex8 if H == 8 else ex4)[:, par, :, 0:H],
                                     back_ps[:, 0:TH].rearrange("p (t h) -> p t h", h=H), ACT.Exp)
                nc.scalar.activation(ex_ps[par][:, 0:TH], back_ps[:, 0:TH], ACT.Exp).then_inc(ex_ready, 1)
                act.wait_ge(resc_ready, n)
                nc.scalar.activation(resc_f[par][:, :], resc_ps, ACT.Copy)
                nc.scalar.activation(resc_h[par][0:H, :], resch_ps[0:H, :], ACT.Copy).then_inc(resc_copied, 1)

            group_loop(act, step)

        def node_act(act, s):
            cb = NCH * (s + 1)
            last = s == last_stage
            with act.Fori(0, NCH) as i:
                cols = bass.ds(i * CH, CH)
                if s == -1:
                    nc.scalar.activation(st[:, :, :], xT[:, :, cols], ACT.Copy).then_inc(st_ready, 1)
                if s > 0:
                    act.wait_ge(to_act, NCH * (s - 1) + i + 1)
                if s == 3:
                    nc.scalar.activation(c[:, 1, :], c[:, 0, :], ACT.Sqrt).then_inc(from_act, 1)
                if s in (1, 2):
                    nc.scalar.activation(st[:, :, :], v[:, :, :], ACT.Relu).then_inc(st_ready, 1)
                if s == 4:
                    for f in range(FC):
                        ins = nc.scalar.activation(t[:, f, :], v[:, f, :], ACT.Relu, bias=bias[:, 4, f:f + 1])
                    ins.then_inc(from_act, 1)
                if s in (5, 6):
                    nc.scalar.activation(t[:, :, :], c[:, :, :], ACT.Exp).then_inc(from_act, 1)
                if s in LN_STAGES:
                    lb = NCH * LN_STAGES.index(s)
                    act.wait_ge(c_ready, lb + i + 1)
                    nc.scalar.activation(t[:, :, :], c[:, :, :], ACT.Square).then_inc(sq_ready, 1)
                    act.wait_ge(var_ready, lb + i + 1)
                    nc.scalar.activation(v[:, 0, :], wide(2)[:, 0:CH], ACT.Sqrt, bias=eps[:, :]).then_inc(std_ready, 1)
                if s in (0, 3, 4, 5) and not last:
                    act.wait_ge(st_ready, cb + i + 1)
                    nc.scalar.activation((rT if s == 5 else xT)[:, :, cols], st[:, :, :], ACT.Copy)
                if s in ROOT_STAGES and not last:
                    act.wait_ge(root_ready, NCH * ROOT_STAGES.index(s) + i + 1)
                    for f in range(FC):
                        if s < 3:
                            ins = nc.scalar.activation(rT[:, f, cols], wide(4 + 2 * f)[:, 0:CH], ACT.Identity,
                                                       bias=bias[:, s + 1, f:f + 1])
                        else:
                            ins = nc.scalar.activation(acc[:, f, cols], wide(4 + 2 * f)[:, 0:CH], ACT.Copy)
                w = D if last else LAYERS[s + 1][2]
                act.wait_ge(tb_free, cb + i + 1)
                for k in range(5):
                    act.wait_ge(row_ready, 5 * cb + 5 * i + k + 1)
                    nc.scalar.activation(tb[:, k, 0:w], ps[:, k % 4, 0:w], ACT.Copy).then_inc(row_out, 1)

        def edge_dve(dve, l, ch, turns):
            V = nc.vector
            kind, H, W = LAYERS[l]
            TH = T * H
            node_reg = dve.alloc_register(f"node{l}")

            def make_onehot(g, k, w=None):
                return V.tensor_scalar(onehot[:, k, :], iota[:, 0:P] if w is None else iota[:, bass.ds(w * P, P)],
                                       local[:, bass.ds(g * T + k, 1)], None, ALU.is_equal)

            def add_window(node):
                if kind != "sum":
                    nd = 9 if H == 8 else H
                    dwin = den[0:nd, bass.ds(node, P)]
                    V.tensor_tensor(dwin, dwin, den_ps[0:nd, :], ALU.add)
                win = acc[:, :, bass.ds(node, P)]
                return V.tensor_tensor(win, win, sums_ps, ALU.add)

            def rescale_node(g, par):
                node = V.value_load(base[0:1, bass.ds(g, 1)], min_val=0, max_val=N)
                dve.wait_ge(ex_ready, ag + g + 1)
                dve.wait_ge(resc_copied, ag + g + 1)
                dve.wait_ge(added, NG * l + g + 1)
                col = acc[:, :, bass.ds(node, 1)]
                V.tensor_tensor(col, col, resc_f[par][:, :].unsqueeze(2), ALU.mult)
                dcol = den[0:H, bass.ds(node, 1)]
                V.tensor_tensor(dcol, dcol, resc_h[par][0:H, :], ALU.mult).then_inc(rescaled, 1)

            def add_group(g):
                node = V.value_load(base[0:1, bass.ds(g, 1)], min_val=0, max_val=N)
                dve.wait_ge(added, NG * l + g + 1)
                if kind != "sum":
                    dve.wait_ge(rescaled, NG * ATT.index(l) + g + 1)
                dve.wait_ge(sum_ready, NG * l + g + 1)
                add_window(node).then_inc(added, 1)

                def window(w):
                    for k in range(T):
                        ins = make_onehot(g, k, w)
                    ins.then_inc(more_ready, 1)
                    start = V.value_load(base[0:1, bass.ds(g, 1)], min_val=0, max_val=N)
                    dve.reg_mov(node_reg, start + w * P)
                    dve.wait_ge(more_summed, turns.now() + 1)
                    add_window(V.snap(node_reg, min_val=0, max_val=N)).then_inc(more_added, 1)
                    dve.wait_ge(more_added, turns.now() + 1)
                    turns.next()
                further_windows(dve, g, window)
                dve.sem_inc(rows_free, 1)

            if kind == "sum":
                def step(g, h, par, first):
                    for k in range(T):
                        make_onehot(g, k).then_inc(tile_ready, 1)
                    add_group(g)

                group_loop(dve, step)
                return

            ag = NG * ATT.index(l)
            grid = lambda x: x[:, 0:TH].rearrange("p (t h) -> p t h", h=H)
            row = lambda x, j: x[0:1, j * H * SLOTS:(j + 1) * H * SLOTS].rearrange("o (h t) -> o h t", h=H)

            def messages(g, par, q):
                if q == 0:
                    rescale_node(g, par)
                for k in (2 * q, 2 * q + 1):
                    make_onehot(g, k)
                    V.tensor_tensor(msg[:, k, :].rearrange("p (h d) -> p h d", h=H),
                                    src_rows(l, par)[:, k, 0:D].rearrange("p (h d) -> p h d", h=H),
                                    ex_ps[par][:, k * H:(k + 1) * H].unsqueeze(2).broadcast_to([P, H, D // H]),
                                    ALU.mult).then_inc(tile_ready, 1)
                if q == 3:
                    add_group(g)

            def step(g, h, par, first):
                n = ag + g + 1
                src = src_rows(l, par)

                def prev_messages(q):
                    if not first:
                        messages(g - 1, 1 - par, q)

                dve.wait_ge(seg_landed[par], SEG_BEFORE[l] + (48 if H == 8 else 32) * (h + 1))
                d = dseg[0:TH, par, :]
                for j in range(2):
                    m = row(marks[:, par, :], j)
                    V.tensor_tensor(row(pen_row, j)[:, :, 1 - j:SLOTS - j], m[:, :, 1:], m[:, :, 0:T], ALU.not_equal)
                ch.then(V.tensor_tensor(pen[0:TH, :], d[:, 1:P + 2], d[:, 0:P + 1], ALU.not_equal))
                for j in range(2):
                    x = row(pen_row, j)[:, :, 1 - j:SLOTS - j]
                    V.tensor_scalar(x, x, -BIG, None, ALU.mult)
                V.tensor_scalar(pen_first[0:TH, :], d[:, 1:P + 1], d[:, 0:1], -BIG, ALU.not_equal, ALU.mult)
                V.tensor_scalar(pen_last[0:TH, :], d[:, 1:P + 1], d[:, P + 1:P + 2], -BIG, ALU.not_equal, ALU.mult)
                pens = ch.done(V.tensor_scalar(pen[0:TH, :], pen[0:TH, :], -BIG, None, ALU.mult))
                if kind == "gat_edge":
                    for hf in range(2):
                        dve.wait_ge(dst_landed[hf], 64 * (g + 1))
                        at = None
                        for k in range(4 * hf, 4 * hf + 5):
                            if k < 4 * hf + 4:
                                dve.wait_ge(enc_ready, g * T + k + 1)
                                now = ch.done(V.scalar_tensor_tensor(prod[:, k % 4, :], enc_ps[k % 2], 0.0,
                                                                     drows[:, hf, k % 4, 0:D], ALU.max, ALU.mult))
                            if at is not None:
                                ch.wait(at)
                                dve.sem_inc(enc_free, 1)
                                red = V.tensor_reduce(grid(al)[:, k - 1, :],
                                                      prod[:, (k - 1) % 4, :].rearrange("p (h d) -> p h d", h=H), AX.X, ALU.add)
                            at = now
                        ch.then(red)
                        ch.then(V.tensor_tensor(grid(al2)[:, 4 * hf:4 * hf + 4, :], grid(al)[:, 4 * hf:4 * hf + 4, :],
                                                drows[:, hf, :, D + 8:D + 16], ALU.add))
                        dve.sem_inc(drows_free, 1)
                    dve.wait_ge(src_landed[par], HALF_TILES * l + (h + 1) * 16 * T)
                    ch.then(V.tensor_tensor(grid(al), grid(al2), src[:, :, D:D + 8], ALU.add))
                else:
                    dve.wait_ge(dst_landed[par], HALF_TILES * ATT.index(l) + (h + 1) * 16 * T)
                    dve.wait_ge(src_landed[par], HALF_TILES * l + (h + 1) * 16 * T)
                    ch.then(V.tensor_tensor(grid(al), dsmall[:, par, :, :], src[:, :, D:D + 4], ALU.add))
                    dve.sem_inc(drows_free, 1)
                dve.sem_inc(seg_free, 1)
                V.scalar_tensor_tensor(al3[:, 0:TH], al[:, 0:TH], 0.2, al[:, 0:TH], ALU.mult, ALU.max).then_inc(al_ready, 1)
                prev_messages(0)
                ch.wait(pens)
                dve.wait_ge(alT_ready, n)
                aT = alT_ps[0:TH, :]
                V.tensor_tensor_scan(fwd[0:TH, :], pen[0:TH, 0:P], aT, -BIG, ALU.add, ALU.max)
                V.tensor_tensor_scan(bwd[0:TH, ::-1], pen[0:TH, 1:P + 1][:, ::-1], aT[:, ::-1], -BIG, ALU.add,
                                     ALU.max).then_inc(scans_ready, 1)
                prev_messages(1)
                dve.wait_ge(last_ready, n)
                V.tensor_copy(row(edge_row, 0)[:, :, 1:], edge_ps[:, 0:TH].rearrange("o (t h) -> o h t", h=H))
                ch.then(V.tensor_copy(row(edge_row, 1)[:, :, 0:T], edge_ps[:, TH:2 * TH].rearrange("o (t h) -> o h t", h=H)))
                HS = H * SLOTS
                V.tensor_tensor_scan(carry_row[0:1, 0:HS], pen_row[0:1, 0:HS], edge_row[0:1, 0:HS], -BIG, ALU.add, ALU.max)
                ch.then(V.tensor_tensor_scan(carry_row[0:1, HS:2 * HS][:, ::-1], pen_row[0:1, HS:2 * HS][:, ::-1],
                                             edge_row[0:1, HS:2 * HS][:, ::-1], -BIG, ALU.add, ALU.max))
                V.tensor_copy(row(edge_row, 0)[:, :, 0:1], row(carry_row, 0)[:, :, T:SLOTS])
                for j in range(2):
                    ins = V.tensor_copy(carry_th[:, j, 0:TH].rearrange("o (t h) -> o h t", h=H), row(carry_row, j)[:, :, j:T + j])
                ins.then_inc(carry_ready, 1)
                dve.wait_ge(scans_ready, n)
                both_ways = ch.done(V.tensor_tensor(segmax[0:TH, :], fwd[0:TH, :], bwd[0:TH, :], ALU.max))
                prev_messages(2)
                ch.wait(both_ways)
                dve.wait_ge(carryT_ready, n)
                for pn, j in ((pen_first, 0), (pen_last, 1)):
                    ch.then(V.scalar_tensor_tensor(segmax[0:TH, :], pn[0:TH, :], carry_ps[0:TH, j:j + 1], segmax[0:TH, :],
                                                   ALU.add, ALU.max))
                V.tensor_tensor(shifted[0:TH, :], aT, segmax[0:TH, :], ALU.subtract)
                V.tensor_scalar(rescale[0:H, :], carry_ps[0:H, 0:1], segmax[0:H, 0:1], 0.0, ALU.subtract,
                                ALU.min).then_inc(shift_ready, 1)
                prev_messages(3)

            V.memset(edge_row[:, :], -BIG)
            ch.then(V.memset(pen_row[:, :], -BIG))
            group_loop(dve, step, per=CHAIN_STEPS[kind], chain=ch)
            for q in range(4):
                messages(NG - 1, 1, q)

        def node_dve(dve, s, ch):
            V = nc.vector
            cb = NCH * (s + 1)
            last = s == last_stage
            dve.wait_ge(added, NG * (s + 1) + 1)
            both = lambda x: x.unsqueeze(1).broadcast_to([P, FC, CH])
            with dve.Fori(0, NCH) as i:
                ch.enter(i, NODE_STEPS[s])
                cols = bass.ds(i * CH, CH)
                dve.wait_ge(st_ready, cb + i)
                if s in ATT:
                    dve.wait_ge(den_bc, NCH * DEN_STAGES.index(s) + i + 1)
                    ch.then(V.tensor_scalar(t[:, :, :], ps[:, 0:4, :].rearrange("p (f b) n -> p f (b n)", f=FC)[:, :, 0:CH],
                                            1e-10 if s == 0 else 1e-30, None, ALU.max))
                    ch.then(V.reciprocal(t[:, :, :], t[:, :, :]))
                    ch.then(V.tensor_tensor(v[:, :, :], acc[:, :, cols], t[:, :, :], ALU.mult))
                    for f in range(FC):
                        ins = V.scalar_tensor_tensor(v[:, f, :], v[:, f, :], bias[:, s, f:f + 1],
                                                     (rT if s == 6 else xT)[:, f, cols], ALU.add, ALU.add)
                    if s == 0:
                        ch.then(V.tensor_scalar(c[:, 1, :], wide(4)[:, 0:CH], 1.0, None, ALU.max))
                        V.reciprocal(norm[:, cols], c[:, 1, :]).then_inc(v_ready, 1)
                    else:
                        ch.then(ins)
                        V.tensor_scalar(c[:, :, :], v[:, :, :], 0.0, None, ALU.min).then_inc(to_act, 1)
                        dve.wait_ge(from_act, NCH * FROM_ACT_STAGES.index(s) + i + 1)
                        if s == 5:
                            dve.wait_ge(row_out, 5 * cb + 5 * i)
                            V.scalar_tensor_tensor(st[:, :, :], t[:, :, :], -1.0, v[:, :, :], ALU.add, ALU.max).then_inc(st_ready, 1)
                        else:
                            ch.then(V.scalar_tensor_tensor(v[:, :, :], t[:, :, :], -1.0, v[:, :, :], ALU.add, ALU.max))
                            V.tensor_tensor(v[:, :, :], v[:, :, :], xT[:, :, cols], ALU.add).then_inc(v_ready, 1)
                elif s == 4:
                    V.tensor_tensor(v[:, :, :], acc[:, :, cols], both(norm[:, cols]), ALU.mult).then_inc(to_act, 1)
                    dve.wait_ge(from_act, NCH * FROM_ACT_STAGES.index(s) + i + 1)
                    V.tensor_tensor(v[:, :, :], t[:, :, :], xT[:, :, cols], ALU.add).then_inc(v_ready, 1)
                else:
                    if s == 3:
                        dve.wait_ge(den_bc, NCH * DEN_STAGES.index(s) + i + 1)
                        V.tensor_scalar(c[:, 0, :], wide(4)[:, 0:CH], 1.0, None, ALU.add).then_inc(to_act, 1)
                    ch.then(V.tensor_tensor(v[:, :, :], acc[:, :, cols], both(norm[:, cols]), ALU.mult))
                    ins = V.tensor_tensor(v[:, :, :], v[:, :, :], rT[:, :, cols], ALU.add)
                    if s < 3:
                        ins.then_inc(to_act, 1)
                        dve.wait_ge(st_ready, cb + i + 1)
                    else:
                        ch.then(ins)
                        V.tensor_tensor(v[:, :, :], v[:, :, :], xT[:, :, cols], ALU.add).then_inc(v_ready, 1)
                        wait_alone(dve, from_act, i + 1)
                        norm_at = ch.done(V.reciprocal(norm[:, cols], c[:, 1, :]))
                if s in LN_STAGES:
                    lb = NCH * LN_STAGES.index(s)
                    dve.wait_ge(mean_ready, lb + i + 1)
                    if s == 3:
                        ch.wait(norm_at)
                    V.tensor_tensor(c[:, :, :], v[:, :, :], both(wide(0)[:, 0:CH]), ALU.subtract).then_inc(c_ready, 1)
                    dve.wait_ge(std_ready, lb + i + 1)
                    ch.then(V.reciprocal(v[:, 1, :], v[:, 0, :]))
                    dve.wait_ge(row_out, 5 * cb + 5 * i)
                    ins = V.tensor_tensor(st[:, :, :], c[:, :, :], both(v[:, 1, :]), ALU.mult)
                    if s == 3:
                        ch.then(ins)
                        ins = V.tensor_tensor(st2[:, :, :], st[:, :, :], both(norm[:, cols]), ALU.mult)
                    ins.then_inc(st_ready, 1)
                ch.leave(NCH)
            if not last:
                if s != 3:
                    V.memset(acc[:, :, :], 0.0)
                if s + 1 in ATT:
                    V.memset(den[:, :], 0.0)

        block = ctx.enter_context(nc.Block())

        @block.sync
        def _(sp):
            n_loads = [0]

            def load(dst, src):
                n_loads[0] += 1
                sp.dma_start(dst, src).then_inc(loaded, 16)

            load(xT[:, :, :], a["xT"].rearrange("(f p) n -> p f n", p=P))
            load(src_idx[:, :], a["src_idx"])
            load(dst_idx[:, :], a["dst_idx"])
            load(base[:, :], a["base_row"].partition_broadcast(P))
            load(last[:, :], a["last_row"])
            load(bias[:, :, :], a["biases"].rearrange("p (l f) -> p l f", f=FC))
            for s in range(NL):
                load(w_table[s][:, :, 0:D], a[f"w_table{s}"].rearrange("(k p) o -> p k o", p=P))
            for s in w_root:
                load(w_root[s][:, :, :], a[f"w_root{s}"].rearrange("(k p) o -> p k o", p=P))
            load(w_edge[:, :], a["w_edge"])
            for n, s in enumerate((0, 5, 6)):
                load(part[n][:, :, 0:D], a[f"w_out{s}"].rearrange("(k p) i -> p k i", p=P))
                load(part[n][:, 0, D:D + 4], a[f"score_cols{s}"])
            assert n_loads[0] * 16 == LOADED, n_loads

            for l in ATT:
                if l >= n_edge_layers:
                    break
                kind, H, _ = LAYERS[l]

                def seg(g, h, par, _first, l=l, kind=kind, H=H):
                    sp.wait_ge(seg_free, NG * ATT.index(l) + g + 1)
                    sp.dma_start(dseg[0:T * H, par, :], a[f"dst_seg{H}"][bass.ds(T * H * g, T * H), :]).then_inc(seg_landed[par], 16)
                    sp.dma_start(marks[0:1, par, 0:2 * H * SLOTS], a[f"dst_mark{H}"][bass.ds(g, 1), :]).then_inc(seg_landed[par], 16)
                    if kind == "gat_edge":
                        sp.dma_start(attr[:, par, :], a["attrT"][:, bass.ds(T * P * g, T * P)]).then_inc(seg_landed[par], 16)

                if l == 0:
                    store_tables(sp, -1)
                    group_loop(sp, seg)
                    for s in range(0, min(4, last_stage) + 1):
                        store_tables(sp, s)
                else:
                    group_loop(sp, seg)
                    store_tables(sp, l)

        @block.gpsimd
        def _(pool):
            one_left = Steps(pool, consts)
            one_left.then(nc.gpsimd.memset(ident[:, :], 0.0))
            one_left.then(nc.gpsimd.affine_select(out=ident[:, :], in_=ident[:, :], compare_op=ALU.not_equal, fill=1.0,
                                                  base=0, pattern=[[-1, P]], channel_multiplier=1))
            one_left.then(nc.gpsimd.iota(iota[:, :], pattern=[[1, T * P]], base=0, channel_multiplier=0,
                                         allow_small_or_imprecise_dtypes=True))

            def band(x, pattern, base, mult, width, base2=None):
                one_left.then(nc.gpsimd.memset(x, 1.0))
                one_left.then(nc.gpsimd.affine_select(out=x, in_=x, compare_op=ALU.is_ge, fill=0.0,
                                                      base=base, pattern=pattern, channel_multiplier=mult))
                one_left.then(nc.gpsimd.affine_select(out=x, in_=x, compare_op=ALU.is_ge, fill=0.0, base=width - 1 - base,
                                                      pattern=[[-s, n] for s, n in pattern], channel_multiplier=-mult))

            for H in (8, 4):
                band(head_of[H][:, :, :], [[P, FC], [1, P]], 0, -(D // H), D // H)
                band(head_col[H][:, :, :], [[P, FC], [-(D // H), H]], 0, 1, D // H)
            band(deg_row[:, :], [[0, P]], -8, 1, 1)
            assert one_left.k == CONSTS
            pool.sem_inc(rows_free, 2)
            pool.sem_inc(drows_free, 2)
            pool.sem_inc(seg_free, 2)
            pool.sem_inc(enc_free, 2)
            pool.sem_inc(tb_free, 1)
            pool.wait_ge(loaded, LOADED)
            ring = Steps(pool, pool_step)
            for l in range(n_edge_layers):
                kind = LAYERS[l][0]
                pool.wait_ge(table_written, TABLE_SEM[l + 1])

                def gather(g, h, par, _first, l=l, kind=kind):
                    pool.wait_ge(rows_free, NG * l + g + 1)
                    at = ring.done(nc.gpsimd.tensor_copy(src_now[:, par, 0:T], src_idx[:, bass.ds(g * T, T)]))
                    if kind != "sum":
                        at = ring.done(nc.gpsimd.tensor_copy(dst_now[:, par, 0:T], dst_idx[:, bass.ds(g * T, T)]))
                    wait_alone(pool, pool_step, at)
                    if kind == "gat":
                        wait_alone(pool, drows_free, DST_BEFORE[l] + g + 1)
                    for k in range(T):
                        if kind == "gat_edge":
                            if k % 4 == 0:
                                wait_alone(pool, drows_free, 2 * g + k // 4 + 1)
                            pool.indirect_dma_start(
                                drows[:, k // 4, k % 4, :], None, tables[l][:, :],
                                bass.IndirectOffsetOnAxis(ap=dst_now[:, par, k:k + 1], axis=0)).then_inc(dst_landed[k // 4], 16)
                        elif kind == "gat":
                            pool.indirect_dma_start(
                                dsmall[:, par, k, :], None, scores[l][:, :],
                                bass.IndirectOffsetOnAxis(ap=dst_now[:, par, k:k + 1], axis=0)).then_inc(dst_landed[par], 16)
                        pool.indirect_dma_start(
                            src_rows(l, par)[:, k, :], None, tables[l][:, :],
                            bass.IndirectOffsetOnAxis(ap=src_now[:, par, k:k + 1], axis=0)).then_inc(src_landed[par], 16)

                group_loop(pool, gather, per=2 if kind != "sum" else 1, chain=ring)

        @block.tensor
        def _(pe):
            mm = nc.tensor.matmul
            pe.wait_ge(loaded, LOADED)
            pe.wait_ge(consts, CONSTS)
            pe.wait_ge(built, 1)
            for n, (s, cols) in enumerate(((0, 16), (5, 8), (6, 8))):
                for m in range(FC):
                    for k in range(FC):
                        ins = mm(ps[:, 3 * m + n, 0:cols], part[n][:, k, m * P:(m + 1) * P],
                                 st[:, k, n * 16:n * 16 + cols], start=k == 0, stop=k == 1)
            ins.then_inc(built_pe, 1)
            pe.wait_ge(built, 2)
            turns = Turns(pe, "pe_turns")
            node_pe(pe, -1)
            for l in range(n_edge_layers):
                edge_pe(pe, l, turns)
                node_pe(pe, l)

        @block.scalar
        def _(act):
            act.wait_ge(loaded, LOADED)
            act.wait_ge(built, 2)
            node_act(act, -1)
            for l in range(n_edge_layers):
                if LAYERS[l][0] != "sum":
                    edge_act(act, l)
                node_act(act, l)

        @block.vector
        def _(dve):
            V = nc.vector
            ch = Steps(dve, dve_step)
            dve.sem_inc(added, 1)
            V.memset(mean_w[:, :], 1.0 / D)
            V.memset(eps[:, :], EPS)
            V.memset(one[:, :], 1.0)
            V.memset(ex8[:, :, :, 8:9], 1.0)
            V.memset(den[:, :], 0.0)
            V.memset(acc[:, :, :], 0.0)
            V.memset(st[:, :, 0:48], 0.0)
            dve.wait_ge(loaded, LOADED)
            dve.wait_ge(consts, CONSTS)
            by_group = lambda x: x[:, :].rearrange("p (g t) -> p g t", t=T)
            V.tensor_tensor(by_group(local), by_group(dst_idx), base[:, :].unsqueeze(2).broadcast_to([P, NG, T]), ALU.subtract)
            ch.then(V.tensor_tensor(windows[:, :], last[:, :], base[0:1, :], ALU.subtract))
            ch.then(V.tensor_scalar(windows[:, :], windows[:, :], 7, None, ALU.arith_shift_right))
            ch.then(V.tensor_scalar(windows[:, :], windows[:, :], 1.0, None, ALU.add))
            for n, H in enumerate((8, 4, 4)):
                for j in range(2):
                    for k in range(FC):
                        ins = V.tensor_scalar(st[:, k, 16 * n + j * H:16 * n + (j + 1) * H], head_col[H][:, k, :],
                                              part[n][:, 0, D + 2 * j + k:D + 2 * j + k + 1], None, ALU.mult)
            ins.then_inc(built, 1)
            dve.wait_ge(built_pe, 1)
            for n, (s, cols) in enumerate(((0, 16), (5, 8), (6, 8))):
                for m in range(FC):
                    ins = V.tensor_copy(w_table[s][:, m, D:D + cols], ps[:, 3 * m + n, 0:cols])
            ins.then_inc(built, 1)
            turns = Turns(dve, "dve_turns")
            ch.flat()
            for l in range(n_edge_layers):
                dve.wait_ge(row_out, 5 * NCH * (l + 1))
                edge_dve(dve, l, ch, turns)
                node_dve(dve, l, ch)


CHAIN_STEPS = {"gat_edge": 20, "gat": 8}
NODE_STEPS = {0: 5, 1: 1, 2: 1, 3: 5, 4: 1, 5: 4, 6: 6}

INS = (["xT", "src_idx", "dst_idx", "base_row", "biases", "w_edge", "attrT"] + [f"w_table{s}" for s in range(NL)]
       + ["w_root1", "w_root2", "w_root3"] + [f"{n}{s}" for s in (0, 5, 6) for n in ("w_out", "score_cols")]
       + ["dst_seg8", "dst_seg4", "dst_mark8", "dst_mark4", "last_row"])


def lay_out(x, src, dst, edge_attr_3, **w):
    import numpy as np
    x, src, dst = np.asarray(x), np.asarray(src), np.asarray(dst)
    o = {}
    o["xT"] = np.zeros((D, NPAD), x.dtype)
    o["xT"][:, :N] = x.T
    dst_p = np.concatenate([np.full(1, -1, dst.dtype), dst, np.full(PAD_E - E + 1, N, dst.dtype)])
    src_p = np.concatenate([src, np.zeros(PAD_E - E, src.dtype)])
    o["src_idx"] = src_p.reshape(TILES, P).T
    o["dst_idx"] = dst_p[1:-1].reshape(TILES, P).T
    o["base_row"] = dst_p[1:-1:T * P]
    o["last_row"] = dst_p[T * P::T * P][None]
    seg = np.stack([dst_p[t * P:t * P + P + 2] for t in range(TILES)])
    ends, starts = dst_p[0::P][:TILES + 1], dst_p[1::P][:TILES + 1]
    for H in (8, 4):
        o[f"dst_seg{H}"] = np.repeat(seg, H, axis=0)
        o[f"dst_mark{H}"] = np.stack([np.concatenate([np.tile(m[g * T:g * T + T + 1], H) for m in (ends, starts)])
                                      for g in range(NG)])
    attr = np.asarray(edge_attr_3)
    o["attrT"] = np.zeros((4, PAD_E), attr.dtype)
    o["attrT"][:3, :E] = attr.T
    o["attrT"][3] = 1
    A = {k: np.asarray(z) for k, z in w.items()}
    o["w_edge"] = np.concatenate([A["L0_gnn_edge_W"].T, A["L0_gnn_edge_b"][None]])
    b = [A["L0_gnn_bias"], A["L1_gnn_b1l"], A["L1_gnn_b2l"], A["L1_gnn_b3l"], A["L2_gnn_b"], A["L3_gnn_b0"], A["L3_gnn_b1"]]
    o["biases"] = np.stack(b).reshape(7 * FC, P).T
    names = ["L0_gnn_W", "L1_gnn_W1l", "L1_gnn_W2l", "L1_gnn_W3l", "L2_gnn_W"]
    for s, n in enumerate(names):
        o[f"w_table{s}"] = A[n].T
    for s, n in ((1, "W1r"), (2, "W2r"), (3, "W3r")):
        o[f"w_root{s}"] = A["L1_gnn_" + n].T
    o["w_table5"], o["w_table6"] = A["L3_gnn_W0"], A["L3_gnn_W1"]
    o["w_out0"], o["w_out5"], o["w_out6"] = A["L0_gnn_W"], A["L3_gnn_W0"].T, A["L3_gnn_W1"].T
    for s, p, q in ((0, "L0_gnn_a_src", "L0_gnn_a_dst"), (5, "L3_gnn_al0", "L3_gnn_ar0"), (6, "L3_gnn_al1", "L3_gnn_ar1")):
        o[f"score_cols{s}"] = np.concatenate([A[p].reshape(FC, P), A[q].reshape(FC, P)]).T
    return o


STOP = None


def kernel(**inputs):
    import numpy as np
    import concourse.bacc as bacc
    from concourse.bass_utils import run_bass_kernel_spmd

    nc = bacc.Bacc("TRN2", target_bir_lowering=False, num_devices=1)
    o = lay_out(**inputs)
    arrays, args = {}, {}
    for name in INS:
        arr = np.ascontiguousarray(o[name])
        arrays[f"in_{name}"] = arr
        args[name] = nc.dram_tensor(f"in_{name}", arr.shape, mybir.dt.from_np(arr.dtype), kind="ExternalInput").ap()
    out = nc.dram_tensor("out_x", (NPAD, D), F32, kind="ExternalOutput").ap()
    gnn_program(nc, args, out, STOP)
    r = run_bass_kernel_spmd(nc, [arrays], core_ids=[0])
    return r.results[0]["out_x"][:N]
```

```python
import concourse.bass as bass
from concourse import mybir
from contextlib import ExitStack


F32 = mybir.dt.float32
I32 = mybir.dt.int32
ALU = mybir.AluOpType
ACT = mybir.ActivationFunctionType
AX = mybir.AxisListType

N, E, D = 3125, 53125, 256
P = 128
FC = D // P
TILES = -(-E // P)
TILES += -TILES % 32
PAD_E = TILES * P
NPAD = -(-N // (5 * P)) * 5 * P
CH = 5 * P
NCH = NPAD // CH
SPLITS = [(0, 512), (512, CH - 512)]
WIDE = NPAD + P
BIG = 1.0e30
EPS = 1e-5
TW = D + 16

T = 8
NG = TILES // T
SLOTS = T + 1
LAYERS = [("gat_edge", 8, D + 16), ("sum", 0, D), ("sum", 0, D), ("sum", 0, D), ("sum", 0, D),
          ("gat", 4, D + 8), ("gat", 4, D + 8)]
NL = len(LAYERS)
ATT = [l for l in range(NL) if LAYERS[l][0] != "sum"]
LN_STAGES = [0, 3, 4, 6]
ROOT_STAGES = [0, 1, 2, 3]
DEN_STAGES = [0, 3, 5, 6]
FROM_ACT_STAGES = [3, 4, 5, 6]
LOADS = 23
LOADED = 16 * LOADS
CONSTS = 3 + 3 * 5
HALF_TILES = 16 * TILES // 2
DST_BEFORE = {5: 2 * NG, 6: 3 * NG}
TABLE_SEM = [16 * NCH * (s + max(0, s - 5)) for s in range(NL + 1)]
SEG_BEFORE = {0: 0, 5: 24 * NG, 6: 40 * NG}


def is_last(g):
    return isinstance(g, int) and g == NG - 1


def gnn_program(nc, a, out, stop):
    last_stage = NL - 1 if stop is None else stop
    ctx = ExitStack()
    with ctx:
        def sb(name, shape, dt=F32):
            return ctx.enter_context(nc.sbuf_tensor(name, shape, dt))

        def sem(name):
            return ctx.enter_context(nc.semaphore(name))

        xT = sb("xT", [P, FC, NPAD])
        rT = sb("rT", [P, FC, NPAD])
        acc = sb("acc", [P, FC, WIDE])
        den = sb("den", [9, NPAD + CH])
        inv = sb("inv", [9, CH])
        floor = sb("floor", [9, 1])
        norm = sb("norm", [P, NPAD])
        w_table = [sb(f"w_table{s}", [P, FC, TW if s in (0, 5, 6) else D]) for s in range(NL)]
        w_root = {s: sb(f"w_root{s}", [P, FC, D]) for s in (1, 2, 3)}
        bias = sb("bias", [P, 7, FC])
        w_edge = sb("w_edge", [4, D])
        ident = sb("ident", [P, P])
        iota = sb("iota", [P, T * P])
        mean_w = sb("mean_w", [P, P])
        eps = sb("eps", [P, 1])
        unit = sb("unit", [P, 1])
        one = sb("one", [1, 1])
        head_of = {8: sb("head_of8", [8, FC, P]), 4: sb("head_of4", [4, FC, P])}
        head_col = {8: sb("head_col8", [P, FC, 8]), 4: sb("head_col4", [P, FC, 4])}
        deg_row = sb("deg_row", [9, P])
        src_idx = sb("src_idx", [P, TILES], I32)
        dst_idx = sb("dst_idx", [P, TILES], I32)
        base = sb("base", [P, NG], I32)
        last = sb("last", [1, NG], I32)
        windows = sb("windows", [1, NG], I32)
        local = sb("local", [P, TILES])
        rows = sb("rows", [P, 4 * T * TW])
        onehot = rows[:, 2 * T * TW:2 * T * TW + T * P].rearrange("p (t n) -> p t n", t=T)
        prod = rows[:, 2 * T * TW + T * P:2 * T * TW + T * P + 4 * D].rearrange("p (t d) -> p t d", t=4)
        msg = rows[:, 4 * T * TW - T * D:4 * T * TW].rearrange("p (t d) -> p t d", t=T)
        drows = sb("drows", [P, 2, 4, TW])
        src_now = sb("src_now", [P, 2, T], I32)
        dst_now = sb("dst_now", [P, 2, T], I32)
        dsmall = sb("dsmall", [P, 2, T, 4])
        attr = sb("attr", [4, 2, T * P])
        al = sb("al", [P, 64])
        al2 = sb("al2", [P, 64])
        al3 = sb("al3", [P, 64])
        dseg = sb("dseg", [64, 2, P + 2], I32)
        marks = sb("marks", [1, 2, 2 * 8 * SLOTS], I32)
        pen = sb("pen", [64, P + 1])
        pen_first = sb("pen_first", [64, P])
        pen_last = sb("pen_last", [64, P])
        pen_row = sb("pen_row", [1, 2 * 8 * SLOTS])
        fwd = sb("fwd", [64, P])
        bwd = sb("bwd", [64, P])
        segmax = sb("segmax", [64, P])
        shifted = sb("shifted", [64, P])
        edge_row = sb("edge_row", [1, 2 * 8 * SLOTS])
        carry_row = sb("carry_row", [1, 2 * 8 * SLOTS])
        carry_th = sb("carry_th", [1, 2, 64])
        rescale = sb("rescale", [8, 1])
        rescale_e = sb("rescale_e", [8, 1])
        resc_f = [sb(f"resc_f{p}", [P, FC]) for p in range(2)]
        resc_h = [sb(f"resc_h{p}", [8, 1]) for p in range(2)]
        ex8 = sb("ex8", [P, 2, T, 9])
        ex4 = sb("ex4", [P, 2, T, 4])
        part = [rows[:, i * FC * CH:(i + 1) * FC * CH].rearrange("p (f n) -> p f n", f=FC) for i in range(5)]
        v, c, t = part[:3]
        st = part[3]
        st2 = part[4]
        tb = rows[:, 5 * FC * CH:5 * FC * CH + 5 * TW].rearrange("p (k w) -> p k w", k=5)

        ps = ctx.enter_context(nc.psum_tensor("ps", [P, 8, 512], F32))
        enc_ps = [ps[:, p, 0:2 * D].rearrange("p (t d) -> p t d", t=2) for p in range(2)]
        sum_ps = [ps[:, 2 + f, 0:P] for f in range(FC)]
        sums_ps = ps[:, 2:4, 0:P]
        den_ps = ps[0:9, 4, 0:P]
        alT_ps = ps[0:64, 5, 0:P]
        carry_ps = ps[0:64, 5, P:P + 2]
        edge_ps = ps[0:1, 5, 192:320]
        back_ps = ps[:, 5, 320:384]
        resc_ps = ps[:, 5, 384:384 + FC]
        resch_ps = ps[0:8, 5, 388:389]
        ex_ps = [ps[:, 6 + p, 0:64] for p in range(2)]

        def wide(b):
            return ps[:, b:b + 2, :].rearrange("p b n -> p (b n)")

        tables = [nc.dram_tensor(f"table{l}", (NPAD, LAYERS[l][2]), F32, kind="Internal").ap() for l in range(NL)]
        scores = {l: nc.dram_tensor(f"scores{l}", (NPAD, 4), F32, kind="Internal").ap() for l in (5, 6)}

        loaded = sem("loaded")
        consts = sem("consts")
        built = sem("built")
        src_landed = [sem("src_landed0"), sem("src_landed1")]
        dst_landed = [sem("dst_landed0"), sem("dst_landed1")]
        rows_free = sem("rows_free")
        drows_free = sem("drows_free")
        seg_landed = [sem("seg_landed0"), sem("seg_landed1")]
        seg_free = sem("seg_free")
        enc_ready = sem("enc_ready")
        enc_free = sem("enc_free")
        tile_ready = sem("tile_ready")
        sum_ready = sem("sum_ready")
        added = sem("added")
        onehot_ready = sem("onehot_ready")
        windows_done = sem("windows_done")
        more_ready = sem("more_ready")
        more_summed = sem("more_summed")
        more_added = sem("more_added")
        rescaled = sem("rescaled")
        al_ready = sem("al_ready")
        alT_ready = sem("alT_ready")
        scans_ready = sem("scans_ready")
        last_ready = sem("last_ready")
        carry_ready = sem("carry_ready")
        carryT_ready = sem("carryT_ready")
        shift_ready = sem("shift_ready")
        back_ready = sem("back_ready")
        ex_ready = sem("ex_ready")
        resc_ready = sem("resc_ready")
        resc_copied = sem("resc_copied")
        dve_step = sem("dve_step")
        act_step = sem("act_step")
        inv_ready = sem("inv_ready")
        den_bc = sem("den_bc")
        v_ready = sem("v_ready")
        mean_ready = sem("mean_ready")
        c_ready = sem("c_ready")
        sq_ready = sem("sq_ready")
        var_ready = sem("var_ready")
        diag_ready = sem("diag_ready")
        rstd_ready = sem("rstd_ready")
        std_ready = sem("std_ready")
        to_act = sem("to_act")
        from_act = sem("from_act")
        st_ready = sem("st_ready")
        root_ready = sem("root_ready")
        row_ready = sem("row_ready")
        row_out = sem("row_out")
        table_written = sem("table_written")
        tb_free = sem("tb_free")
        passed = sem("passed")
        built_pe = sem("built_pe")
        pool_step = sem("pool_step")
        out_written = sem("out_written")

        class Steps:

            def __init__(self, eng, s):
                self.eng, self.s, self.base, self.k, self.i, self.per = eng, s, 0, 0, 0, 0

            def enter(self, i, per):
                self.i, self.per, self.k = i, per, 0

            def leave(self, turns):
                assert self.k == self.per, (self.k, self.per)
                self.base += turns * self.per
                self.i, self.per, self.k = 0, 0, 0

            def done(self, ins):
                self.k += 1
                ins.then_inc(self.s, 1)
                return self.base + self.i * self.per + self.k

            def wait(self, at):
                self.eng.wait_ge(self.s, at)

            def then(self, ins):
                self.wait(self.done(ins))

            def flat(self):
                self.base += self.k
                self.k = 0

        n_edge_layers = last_stage + 1

        def wait_alone(eng, s, value):
            eng.wait_ge(s, value)
            eng.sem_inc(passed, 1)

        def group_loop(eng, step, done=lambda: None, per=None, chain=None):
            step(0, 0, 0, True)
            if chain:
                chain.flat()
            with eng.Fori(0, NG // 2 - 1) as i:
                if chain:
                    chain.enter(i, 2 * per)
                step(2 * i + 1, i, 1, False)
                step(2 * i + 2, i + 1, 0, False)
                if chain:
                    chain.leave(NG // 2 - 1)
            step(NG - 1, NG // 2 - 1, 1, False)
            if chain:
                chain.flat()

        class Turns:

            def __init__(self, eng, name):
                self.eng, self.reg = eng, eng.alloc_register(name)
                eng.reg_mov(self.reg, 0)

            def now(self):
                return self.eng.snap(self.reg, min_val=0, max_val=NL * (NG + N // P + 1))

            def next(self):
                self.eng.reg_add(self.reg, self.reg, 1)

        def further_windows(eng, g, body):
            n = eng.value_load(windows[0:1, bass.ds(g, 1)], min_val=1, max_val=T)
            with eng.If(n > 1):
                with eng.Fori(1, n) as w:
                    body(w)
            eng.end_ifs()

        def store_tables(sp, s):
            last = s == last_stage
            with sp.Fori(0, NCH) as i:
                sp.wait_ge(row_out, 5 * NCH * (s + 1) + 5 * i + 5)
                if last:
                    sp.dma_start(out[bass.ds(i * CH, CH), :].rearrange("(k p) w -> p k w", p=P),
                                 tb[:, :, 0:D]).then_inc(out_written, 16)
                    sp.wait_ge(out_written, 16 * i + 16)
                    sp.sem_inc(tb_free, 1)
                else:
                    w = LAYERS[s + 1][2]
                    sp.dma_start(tables[s + 1][bass.ds(i * CH, CH), :].rearrange("(k p) w -> p k w", p=P),
                                 tb[:, :, 0:w]).then_inc(table_written, 16)
                    if s + 1 in scores:
                        sp.dma_start(scores[s + 1][bass.ds(i * CH, CH), :].rearrange("(k p) w -> p k w", p=P),
                                     tb[:, :, D + 4:D + 8]).then_inc(table_written, 16)
                    sp.wait_ge(table_written, TABLE_SEM[s + 1] + (TABLE_SEM[s + 2] - TABLE_SEM[s + 1]) // NCH * (i + 1))
                    sp.sem_inc(tb_free, 1)

        def src_rows(l, par):
            W = LAYERS[l][2]
            return rows[:, par * T * TW:par * T * TW + T * W].rearrange("p (t w) -> p t w", t=T)

        def edge_pe(pe, l, turns):
            kind, H, W = LAYERS[l]
            mm = nc.tensor.matmul
            TH = T * H
            pe.wait_ge(row_out, 5 * NCH * (l + 1))

            def tile_sums(par, k):
                lhs = src_rows(l, par)[:, k, 0:D] if kind == "sum" else msg[:, k, :]
                for f in range(FC):
                    ins = mm(sum_ps[f], lhs[:, f * P:(f + 1) * P], onehot[:, k, :], start=k == 0, stop=k == T - 1)
                if kind != "sum":
                    ex = (ex8 if H == 8 else ex4)[:, par, k, :]
                    ins = mm(den_ps[0:ex.shape[-1], :], ex, onehot[:, k, :], start=k == 0, stop=k == T - 1)
                return ins

            def sums(g, par, k):
                if kind != "sum" and k == 0:
                    pe.wait_ge(onehot_ready, NG * ATT.index(l) + g + 1)
                pe.wait_ge(tile_ready, TILES * l + g * T + k + 1)
                ins = tile_sums(par, k)
                if k == T - 1:
                    ins.then_inc(sum_ready, 1)

                    def window(w):
                        pe.wait_ge(more_ready, turns.now() + 1)
                        for kk in range(T):
                            more = tile_sums(par, kk)
                        more.then_inc(more_summed, 1)
                        turns.next()
                    further_windows(pe, g, window)

            if kind == "sum":
                def step(g, h, par, _first):
                    pe.wait_ge(src_landed[par], HALF_TILES * l + (h + 1) * 16 * T)
                    for k in range(T):
                        sums(g, par, k)
                group_loop(pe, step)
                return

            ag = NG * ATT.index(l)

            def encode(g, h, par, half):
                pe.wait_ge(seg_landed[par], 48 * (h + 1))
                for q in range(2):
                    pe.wait_ge(enc_free, g * T // 2 + 2 * half + q + 1)
                    for j in range(2):
                        k = 4 * half + 2 * q + j
                        ins = mm(enc_ps[q][:, j, :], attr[:, par, k * P:(k + 1) * P], w_edge[:, :], start=True, stop=True)
                    ins.then_inc(enc_ready, 1)

            def step(g, h, par, first):
                n = ag + g + 1
                if kind == "gat_edge":
                    if first:
                        encode(g, h, par, 0)
                        encode(g, h, par, 1)
                if not (first and l == 0):
                    pe.wait_ge(resc_copied, n - 1)
                wait_alone(pe, al_ready, n)
                nc.tensor.transpose(alT_ps[0:TH, :], al3[:, 0:TH], ident[:, :]).then_inc(alT_ready, 1)
                if kind == "gat_edge" and not is_last(g):
                    encode(g + 1, h + par, 1 - par, 0)
                wait_alone(pe, scans_ready, n)
                mm(edge_ps[:, 0:TH], fwd[0:TH, P - 1:P], ident[0:TH, 0:TH], start=True, stop=True)
                mm(edge_ps[:, TH:2 * TH], bwd[0:TH, 0:1], ident[0:TH, 0:TH], start=True, stop=True).then_inc(last_ready, 1)
                if kind == "gat_edge" and not is_last(g):
                    encode(g + 1, h + par, 1 - par, 1)
                wait_alone(pe, carry_ready, n)
                for j in range(2):
                    ins = mm(carry_ps[0:TH, j:j + 1], carry_th[:, j, 0:TH], one[:, :], start=True, stop=True)
                ins.then_inc(carryT_ready, 1)
                wait_alone(pe, shift_ready, n)
                nc.tensor.transpose(back_ps[:, 0:TH], shifted[0:TH, :], ident[0:TH, 0:TH]).then_inc(back_ready, 1)
                wait_alone(pe, ex_ready, n)
                for f in range(FC):
                    mm(resc_ps[:, f:f + 1], head_of[H][:, f, :], rescale_e[0:H, :], start=True, stop=True)
                mm(resch_ps[0:H, :], ident[0:H, 0:H], rescale_e[0:H, :], start=True, stop=True).then_inc(resc_ready, 1)
                for k in range(T):
                    sums(g, par, k)

            group_loop(pe, step)

        def node_pe(pe, s):
            mm = nc.tensor.matmul
            cb = NCH * (s + 1)
            last = s == last_stage
            if s >= 0:
                pe.wait_ge(added, NG * (s + 1) + 1)
                pe.wait_ge(windows_done, NG * (s + 1))
            with pe.Fori(0, NCH) as i:
                if s >= 0:
                    pe.wait_ge(row_out, 5 * cb + 5 * i)
                if s in ATT:
                    H = LAYERS[s][1]
                    pe.wait_ge(inv_ready, (NCH + 1) * ATT.index(s) + i + 1)
                    for lo, n in SPLITS:
                        for f in range(FC):
                            ins = mm(wide(2 * f)[:, lo:lo + n], head_of[H][:, f, :], inv[0:H, lo:lo + n],
                                     start=True, stop=True)
                if s == 0:
                    for lo, n in SPLITS:
                        ins = mm(wide(4)[:, lo:lo + n], deg_row[:, :], inv[:, lo:lo + n], start=True, stop=True)
                if s == 3:
                    for lo, n in SPLITS:
                        ins = mm(wide(4)[:, lo:lo + n], deg_row[:, :], den[0:9, bass.ds(i * CH + lo, n)],
                                 start=True, stop=True)
                if s in DEN_STAGES:
                    ins.then_inc(den_bc, 1)
                if s in LN_STAGES:
                    lb = NCH * LN_STAGES.index(s)
                    pe.wait_ge(v_ready, lb + i + 1)
                    for lo, n in SPLITS:
                        for f in range(FC):
                            ins = mm(wide(0)[:, lo:lo + n], mean_w[:, :], v[:, f, lo:lo + n], start=f == 0, stop=f == 1)
                    ins.then_inc(mean_ready, 1)
                    pe.wait_ge(sq_ready, lb + i + 1)
                    for k in range(5):
                        for f in range(FC):
                            ins = mm(ps[:, 2, k:k + 1], t[:, f, k * P:(k + 1) * P], mean_w[:, 0:1],
                                     start=f == 0, stop=f == 1)
                    ins.then_inc(var_ready, 1)
                    pe.wait_ge(diag_ready, lb + i + 1)
                    for lo, n in SPLITS:
                        ins = mm(wide(2)[:, lo:lo + n], mean_w[:, :], v[:, 1, lo:lo + n], start=True, stop=True)
                    ins.then_inc(rstd_ready, 1)
                pe.wait_ge(st_ready, cb + i + 1)
                x = st2 if s == 3 else st
                if s in ROOT_STAGES and not last:
                    rb = NCH * ROOT_STAGES.index(s)
                    w = w_root[s + 1] if s < 3 else w_table[4]
                    for f in range(FC):
                        for lo, n in SPLITS:
                            for k in range(FC):
                                ins = mm(wide(4 + 2 * f)[:, lo:lo + n], w[:, k, f * P:(f + 1) * P],
                                         x[:, k, lo:lo + n], start=k == 0, stop=k == 1)
                    ins.then_inc(root_ready, 1)
                for k in range(5):
                    b = k % 4
                    if k == 4:
                        pe.wait_ge(row_out, 5 * cb + 5 * i + 1)
                    if last:
                        for f in range(FC):
                            ins = nc.tensor.transpose(ps[:, b, f * P:(f + 1) * P], st[:, f, k * P:(k + 1) * P], ident[:, :])
                    else:
                        w = LAYERS[s + 1][2]
                        for f in range(FC):
                            ins = mm(ps[:, b, 0:w], x[:, f, k * P:(k + 1) * P], w_table[s + 1][:, f, 0:w],
                                     start=f == 0, stop=f == 1)
                    ins.then_inc(row_ready, 1)

        def edge_act(act, l, ch):
            H = LAYERS[l][1]
            TH = T * H

            def step(g, h, par, first):
                n = NG * ATT.index(l) + g + 1
                if l == 0 and first:
                    act.wait_ge(consts, CONSTS)
                else:
                    act.wait_ge(windows_done, NG * l + g)
                for k in range(T):
                    ins = nc.scalar.activation(onehot[:, k, :], iota[:, 0:P], ACT.Abs, scale=-1.0,
                                               bias=local[:, bass.ds(g * T + k, 1)])
                distances = ch.done(ins)
                ch.wait(distances)
                nc.scalar.activation(onehot, onehot, ACT.Relu, scale=-1.0, bias=unit[:, :]).then_inc(onehot_ready, 1)
                act.wait_ge(shift_ready, n)
                nc.scalar.activation(rescale_e[0:H, :], rescale[0:H, :], ACT.Exp)
                act.wait_ge(back_ready, n)
                nc.scalar.activation((ex8 if H == 8 else ex4)[:, par, :, 0:H],
                                     back_ps[:, 0:TH].rearrange("p (t h) -> p t h", h=H), ACT.Exp)
                nc.scalar.activation(ex_ps[par][:, 0:TH], back_ps[:, 0:TH], ACT.Exp).then_inc(ex_ready, 1)
                act.wait_ge(resc_ready, n)
                nc.scalar.activation(resc_f[par][:, :], resc_ps, ACT.Copy)
                nc.scalar.activation(resc_h[par][0:H, :], resch_ps[0:H, :], ACT.Copy).then_inc(resc_copied, 1)

            group_loop(act, step, per=1, chain=ch)

        def node_act(act, s):
            cb = NCH * (s + 1)
            last = s == last_stage
            with act.Fori(0, NCH) as i:
                cols = bass.ds(i * CH, CH)
                if s == -1:
                    nc.scalar.activation(st[:, :, :], xT[:, :, cols], ACT.Copy).then_inc(st_ready, 1)
                if s == 0:
                    act.wait_ge(v_ready, i + 1)
                    nc.scalar.activation(norm[:, cols], wide(4)[:, 0:CH], ACT.Copy)
                if s > 0:
                    act.wait_ge(to_act, NCH * (s - 1) + i + 1)
                if s == 3:
                    nc.scalar.activation(c[:, 1, :], c[:, 0, :], ACT.Sqrt).then_inc(from_act, 1)
                if s in (1, 2):
                    nc.scalar.activation(st[:, :, :], v[:, :, :], ACT.Relu).then_inc(st_ready, 1)
                if s == 4:
                    for f in range(FC):
                        ins = nc.scalar.activation(t[:, f, :], v[:, f, :], ACT.Relu, bias=bias[:, 4, f:f + 1])
                    ins.then_inc(from_act, 1)
                if s in (5, 6):
                    nc.scalar.activation(t[:, :, :], c[:, :, :], ACT.Exp).then_inc(from_act, 1)
                if s in LN_STAGES:
                    lb = NCH * LN_STAGES.index(s)
                    act.wait_ge(c_ready, lb + i + 1)
                    nc.scalar.activation(t[:, :, :], c[:, :, :], ACT.Square).then_inc(sq_ready, 1)
                    act.wait_ge(var_ready, lb + i + 1)
                    nc.scalar.activation(v[:, 0, 0:5], ps[:, 2, 0:5], ACT.Sqrt, bias=eps[:, :]).then_inc(std_ready, 1)
                if s in (0, 3, 4, 5) and not last:
                    act.wait_ge(st_ready, cb + i + 1)
                    nc.scalar.activation((rT if s == 5 else xT)[:, :, cols], st[:, :, :], ACT.Copy)
                if s in ROOT_STAGES and not last:
                    act.wait_ge(root_ready, NCH * ROOT_STAGES.index(s) + i + 1)
                    for f in range(FC):
                        if s < 3:
                            ins = nc.scalar.activation(rT[:, f, cols], wide(4 + 2 * f)[:, 0:CH], ACT.Identity,
                                                       bias=bias[:, s + 1, f:f + 1])
                        else:
                            ins = nc.scalar.activation(acc[:, f, cols], wide(4 + 2 * f)[:, 0:CH], ACT.Copy)
                w = D if last else LAYERS[s + 1][2]
                act.wait_ge(tb_free, cb + i + 1)
                for k in range(5):
                    act.wait_ge(row_ready, 5 * cb + 5 * i + k + 1)
                    nc.scalar.activation(tb[:, k, 0:w], ps[:, k % 4, 0:w], ACT.Copy).then_inc(row_out, 1)

        def edge_dve(dve, l, ch, turns):
            V = nc.vector
            kind, H, W = LAYERS[l]
            TH = T * H
            node_reg = dve.alloc_register(f"node{l}")

            def make_onehot(g, k, w=None):
                return V.tensor_scalar(onehot[:, k, :], iota[:, 0:P] if w is None else iota[:, bass.ds(w * P, P)],
                                       local[:, bass.ds(g * T + k, 1)], None, ALU.is_equal)

            def add_window(node):
                if kind != "sum":
                    nd = 9 if H == 8 else H
                    dwin = den[0:nd, bass.ds(node, P)]
                    V.tensor_tensor(dwin, dwin, den_ps[0:nd, :], ALU.add)
                win = acc[:, :, bass.ds(node, P)]
                return V.tensor_tensor(win, win, sums_ps, ALU.add)

            def rescale_node(g, par):
                node = V.value_load(base[0:1, bass.ds(g, 1)], min_val=0, max_val=N)
                dve.wait_ge(resc_copied, ag + g + 1)
                dve.wait_ge(added, NG * l + g + 1)
                col = acc[:, :, bass.ds(node, 1)]
                V.tensor_tensor(col, col, resc_f[par][:, :].unsqueeze(2), ALU.mult)
                dcol = den[0:H, bass.ds(node, 1)]
                V.tensor_tensor(dcol, dcol, resc_h[par][0:H, :], ALU.mult).then_inc(rescaled, 1)

            def add_group(g):
                node = V.value_load(base[0:1, bass.ds(g, 1)], min_val=0, max_val=N)
                dve.wait_ge(added, NG * l + g + 1)
                if kind != "sum":
                    dve.wait_ge(rescaled, NG * ATT.index(l) + g + 1)
                dve.wait_ge(sum_ready, NG * l + g + 1)
                add_window(node).then_inc(added, 1)

                def window(w):
                    for k in range(T):
                        ins = make_onehot(g, k, w)
                    ins.then_inc(more_ready, 1)
                    start = V.value_load(base[0:1, bass.ds(g, 1)], min_val=0, max_val=N)
                    dve.reg_mov(node_reg, start + w * P)
                    dve.wait_ge(more_summed, turns.now() + 1)
                    add_window(V.snap(node_reg, min_val=0, max_val=N)).then_inc(more_added, 1)
                    dve.wait_ge(more_added, turns.now() + 1)
                    turns.next()
                further_windows(dve, g, window)
                dve.sem_inc(windows_done, 1)
                if kind == "sum":
                    dve.sem_inc(rows_free, 1)

            if kind == "sum":
                def step(g, h, par, first):
                    for k in range(T):
                        make_onehot(g, k).then_inc(tile_ready, 1)
                    add_group(g)

                group_loop(dve, step)
                return

            ag = NG * ATT.index(l)
            grid = lambda x: x[:, 0:TH].rearrange("p (t h) -> p t h", h=H)
            row = lambda x, j: x[0:1, j * H * SLOTS:(j + 1) * H * SLOTS].rearrange("o (h t) -> o h t", h=H)

            def messages(g, par):
                dve.wait_ge(ex_ready, ag + g + 1)
                for k in range(T):
                    V.tensor_tensor(msg[:, k, :].rearrange("p (h d) -> p h d", h=H),
                                    src_rows(l, par)[:, k, 0:D].rearrange("p (h d) -> p h d", h=H),
                                    ex_ps[par][:, k * H:(k + 1) * H].unsqueeze(2).broadcast_to([P, H, D // H]),
                                    ALU.mult).then_inc(tile_ready, 1)
                dve.wait_ge(tile_ready, TILES * l + T * g + T)
                dve.sem_inc(rows_free, 1)
                rescale_node(g, par)

            def score_half(g, hf):
                dve.wait_ge(dst_landed[hf], 64 * (g + 1))
                products = []
                for q in range(2):
                    dve.wait_ge(enc_ready, g * T // 2 + 2 * hf + q + 1)
                    products.append(ch.done(V.scalar_tensor_tensor(
                        prod[:, 2 * q:2 * q + 2, :], enc_ps[q], 0.0, drows[:, hf, 2 * q:2 * q + 2, 0:D], ALU.max, ALU.mult)))
                for q in range(2):
                    ch.wait(products[q])
                    dve.sem_inc(enc_free, 1)
                    red = V.tensor_reduce(grid(al)[:, 4 * hf + 2 * q:4 * hf + 2 * q + 2, :],
                                          prod[:, 2 * q:2 * q + 2, :].rearrange("p t (h d) -> p t h d", h=H), AX.X, ALU.add)
                ch.then(red)
                ch.then(V.tensor_tensor(grid(al2)[:, 4 * hf:4 * hf + 4, :], grid(al)[:, 4 * hf:4 * hf + 4, :],
                                        drows[:, hf, :, D + 8:D + 16], ALU.add))
                dve.sem_inc(drows_free, 1)

            def step(g, h, par, first):
                n = ag + g + 1
                src = src_rows(l, par)

                dve.wait_ge(seg_landed[par], SEG_BEFORE[l] + (48 if H == 8 else 32) * (h + 1))
                d = dseg[0:TH, par, :]
                for j in range(2):
                    m = row(marks[:, par, :], j)
                    V.tensor_tensor(row(pen_row, j)[:, :, 1 - j:SLOTS - j], m[:, :, 1:], m[:, :, 0:T], ALU.not_equal)
                ch.then(V.tensor_tensor(pen[0:TH, :], d[:, 1:P + 2], d[:, 0:P + 1], ALU.not_equal))
                for j in range(2):
                    x = row(pen_row, j)[:, :, 1 - j:SLOTS - j]
                    V.tensor_scalar(x, x, -BIG, None, ALU.mult)
                V.tensor_scalar(pen_first[0:TH, :], d[:, 1:P + 1], d[:, 0:1], -BIG, ALU.not_equal, ALU.mult)
                V.tensor_scalar(pen_last[0:TH, :], d[:, 1:P + 1], d[:, P + 1:P + 2], -BIG, ALU.not_equal, ALU.mult)
                pens = ch.done(V.tensor_scalar(pen[0:TH, :], pen[0:TH, :], -BIG, None, ALU.mult))
                if kind == "gat_edge":
                    if first:
                        score_half(g, 0)
                    score_half(g, 1)
                    dve.wait_ge(src_landed[par], HALF_TILES * l + (h + 1) * 16 * T)
                    ch.then(V.tensor_tensor(grid(al), grid(al2), src[:, :, D:D + 8], ALU.add))
                else:
                    dve.wait_ge(dst_landed[par], HALF_TILES * ATT.index(l) + (h + 1) * 16 * T)
                    dve.wait_ge(src_landed[par], HALF_TILES * l + (h + 1) * 16 * T)
                    ch.then(V.tensor_tensor(grid(al), dsmall[:, par, :, :], src[:, :, D:D + 4], ALU.add))
                    dve.sem_inc(drows_free, 1)
                dve.sem_inc(seg_free, 1)
                V.scalar_tensor_tensor(al3[:, 0:TH], al[:, 0:TH], 0.2, al[:, 0:TH], ALU.mult, ALU.max).then_inc(al_ready, 1)
                if not first:
                    add_group(g - 1)
                ch.wait(pens)
                dve.wait_ge(alT_ready, n)
                aT = alT_ps[0:TH, :]
                V.tensor_tensor_scan(fwd[0:TH, :], pen[0:TH, 0:P], aT, -BIG, ALU.add, ALU.max)
                V.tensor_tensor_scan(bwd[0:TH, ::-1], pen[0:TH, 1:P + 1][:, ::-1], aT[:, ::-1], -BIG, ALU.add,
                                     ALU.max).then_inc(scans_ready, 1)
                if kind == "gat_edge" and not is_last(g):
                    score_half(g + 1, 0)
                dve.wait_ge(last_ready, n)
                V.tensor_copy(row(edge_row, 0)[:, :, 1:], edge_ps[:, 0:TH].rearrange("o (t h) -> o h t", h=H))
                ch.then(V.tensor_copy(row(edge_row, 1)[:, :, 0:T], edge_ps[:, TH:2 * TH].rearrange("o (t h) -> o h t", h=H)))
                HS = H * SLOTS
                V.tensor_tensor_scan(carry_row[0:1, 0:HS], pen_row[0:1, 0:HS], edge_row[0:1, 0:HS], -BIG, ALU.add, ALU.max)
                ch.then(V.tensor_tensor_scan(carry_row[0:1, HS:2 * HS][:, ::-1], pen_row[0:1, HS:2 * HS][:, ::-1],
                                             edge_row[0:1, HS:2 * HS][:, ::-1], -BIG, ALU.add, ALU.max))
                V.tensor_copy(row(edge_row, 0)[:, :, 0:1], row(carry_row, 0)[:, :, T:SLOTS])
                for j in range(2):
                    ins = V.tensor_copy(carry_th[:, j, 0:TH].rearrange("o (t h) -> o h t", h=H), row(carry_row, j)[:, :, j:T + j])
                ins.then_inc(carry_ready, 1)
                dve.wait_ge(scans_ready, n)
                both_ways = ch.done(V.tensor_tensor(segmax[0:TH, :], fwd[0:TH, :], bwd[0:TH, :], ALU.max))
                ch.wait(both_ways)
                dve.wait_ge(carryT_ready, n)
                for pn, j in ((pen_first, 0), (pen_last, 1)):
                    ch.then(V.scalar_tensor_tensor(segmax[0:TH, :], pn[0:TH, :], carry_ps[0:TH, j:j + 1], segmax[0:TH, :],
                                                   ALU.add, ALU.max))
                V.tensor_tensor(shifted[0:TH, :], aT, segmax[0:TH, :], ALU.subtract)
                V.tensor_scalar(rescale[0:H, :], carry_ps[0:H, 0:1], segmax[0:H, 0:1], 0.0, ALU.subtract,
                                ALU.min).then_inc(shift_ready, 1)
                messages(g, par)

            V.memset(edge_row[:, :], -BIG)
            ch.then(V.memset(pen_row[:, :], -BIG))
            group_loop(dve, step, per=CHAIN_STEPS[kind], chain=ch)
            add_group(NG - 1)

        def node_dve(dve, s, ch):
            V = nc.vector
            cb = NCH * (s + 1)
            last = s == last_stage
            dve.wait_ge(added, NG * (s + 1) + 1)
            both = lambda x: x.unsqueeze(1).broadcast_to([P, FC, CH])
            rows_of = slice(0, 9 if s == 0 else LAYERS[s][1])

            def reciprocals(lo):
                ch.then(V.tensor_scalar(inv[rows_of, :], den[rows_of, lo], floor[rows_of, :] if s == 0 else 1e-30,
                                        None, ALU.max))
                V.reciprocal(inv[rows_of, :], inv[rows_of, :]).then_inc(inv_ready, 1)

            if s in ATT:
                reciprocals(slice(0, CH))
                ch.flat()
            with dve.Fori(0, NCH) as i:
                ch.enter(i, NODE_STEPS[s])
                cols = bass.ds(i * CH, CH)
                dve.wait_ge(st_ready, cb + i)
                if s in ATT:
                    dve.wait_ge(den_bc, NCH * DEN_STAGES.index(s) + i + 1)
                    ch.then(V.tensor_tensor(v[:, :, :], acc[:, :, cols],
                                            ps[:, 0:4, :].rearrange("p (f b) n -> p f (b n)", f=FC)[:, :, 0:CH], ALU.mult))
                    for f in range(FC):
                        ins = V.scalar_tensor_tensor(v[:, f, :], v[:, f, :], bias[:, s, f:f + 1],
                                                     (rT if s == 6 else xT)[:, f, cols], ALU.add, ALU.add)
                    if s == 0:
                        ins.then_inc(v_ready, 1)
                    else:
                        ch.then(ins)
                        V.tensor_scalar(c[:, :, :], v[:, :, :], 0.0, None, ALU.min).then_inc(to_act, 1)
                        dve.wait_ge(from_act, NCH * FROM_ACT_STAGES.index(s) + i + 1)
                        if s == 5:
                            dve.wait_ge(row_out, 5 * cb + 5 * i)
                            V.scalar_tensor_tensor(st[:, :, :], t[:, :, :], -1.0, v[:, :, :], ALU.add, ALU.max).then_inc(st_ready, 1)
                        else:
                            ch.then(V.scalar_tensor_tensor(v[:, :, :], t[:, :, :], -1.0, v[:, :, :], ALU.add, ALU.max))
                            V.tensor_tensor(v[:, :, :], v[:, :, :], xT[:, :, cols], ALU.add).then_inc(v_ready, 1)
                elif s == 4:
                    V.tensor_tensor(v[:, :, :], acc[:, :, cols], both(norm[:, cols]), ALU.mult).then_inc(to_act, 1)
                    dve.wait_ge(from_act, NCH * FROM_ACT_STAGES.index(s) + i + 1)
                    V.tensor_tensor(v[:, :, :], t[:, :, :], xT[:, :, cols], ALU.add).then_inc(v_ready, 1)
                else:
                    if s == 3:
                        dve.wait_ge(den_bc, NCH * DEN_STAGES.index(s) + i + 1)
                        V.tensor_scalar(c[:, 0, :], wide(4)[:, 0:CH], 1.0, None, ALU.add).then_inc(to_act, 1)
                    ch.then(V.tensor_tensor(v[:, :, :], acc[:, :, cols], both(norm[:, cols]), ALU.mult))
                    ins = V.tensor_tensor(v[:, :, :], v[:, :, :], rT[:, :, cols], ALU.add)
                    if s < 3:
                        ins.then_inc(to_act, 1)
                        dve.wait_ge(st_ready, cb + i + 1)
                    else:
                        ch.then(ins)
                        V.tensor_tensor(v[:, :, :], v[:, :, :], xT[:, :, cols], ALU.add).then_inc(v_ready, 1)
                        wait_alone(dve, from_act, i + 1)
                        norm_at = ch.done(V.reciprocal(norm[:, cols], c[:, 1, :]))
                if s in LN_STAGES:
                    lb = NCH * LN_STAGES.index(s)
                    dve.wait_ge(mean_ready, lb + i + 1)
                    if s == 3:
                        ch.wait(norm_at)
                    V.tensor_tensor(c[:, :, :], v[:, :, :], both(wide(0)[:, 0:CH]), ALU.subtract).then_inc(c_ready, 1)
                    dve.wait_ge(std_ready, lb + i + 1)
                    ch.then(V.reciprocal(v[:, 0, 8:13], v[:, 0, 0:5]))
                    V.scalar_tensor_tensor(v[:, 1, :].rearrange("p (k n) -> p k n", k=5),
                                           ident[:, :].unsqueeze(1).broadcast_to([P, 5, P]), float(D),
                                           v[:, 0, 8:13].unsqueeze(2).broadcast_to([P, 5, P]),
                                           ALU.mult, ALU.mult).then_inc(diag_ready, 1)
                    dve.wait_ge(rstd_ready, lb + i + 1)
                    dve.wait_ge(row_out, 5 * cb + 5 * i)
                    ins = V.tensor_tensor(st[:, :, :], c[:, :, :], both(wide(2)[:, 0:CH]), ALU.mult)
                    if s == 3:
                        ch.then(ins)
                        ins = V.tensor_tensor(st2[:, :, :], st[:, :, :], both(norm[:, cols]), ALU.mult)
                    ins.then_inc(st_ready, 1)
                if s in ATT:
                    reciprocals(bass.ds((i + 1) * CH, CH))
                ch.leave(NCH)
            if not last:
                if s != 3:
                    V.memset(acc[:, :, :], 0.0)
                if s + 1 in ATT:
                    V.memset(den[:, :], 0.0)

        block = ctx.enter_context(nc.Block())

        @block.sync
        def _(sp):
            n_loads = [0]

            def load(dst, src):
                n_loads[0] += 1
                sp.dma_start(dst, src).then_inc(loaded, 16)

            load(xT[:, :, :], a["xT"].rearrange("(f p) n -> p f n", p=P))
            load(src_idx[:, :], a["src_idx"])
            load(dst_idx[:, :], a["dst_idx"])
            load(base[:, :], a["base_row"].partition_broadcast(P))
            load(last[:, :], a["last_row"])
            load(bias[:, :, :], a["biases"].rearrange("p (l f) -> p l f", f=FC))
            for s in range(NL):
                load(w_table[s][:, :, 0:D], a[f"w_table{s}"].rearrange("(k p) o -> p k o", p=P))
            for s in w_root:
                load(w_root[s][:, :, :], a[f"w_root{s}"].rearrange("(k p) o -> p k o", p=P))
            load(w_edge[:, :], a["w_edge"])
            for n, s in enumerate((0, 5, 6)):
                load(part[n][:, :, 0:D], a[f"w_out{s}"].rearrange("(k p) i -> p k i", p=P))
                load(part[n][:, 0, D:D + 4], a[f"score_cols{s}"])
            assert n_loads[0] * 16 == LOADED, n_loads

            for l in ATT:
                if l >= n_edge_layers:
                    break
                kind, H, _ = LAYERS[l]

                def seg(g, h, par, _first, l=l, kind=kind, H=H):
                    sp.wait_ge(seg_free, NG * ATT.index(l) + g + 1)
                    sp.dma_start(dseg[0:T * H, par, :], a[f"dst_seg{H}"][bass.ds(T * H * g, T * H), :]).then_inc(seg_landed[par], 16)
                    sp.dma_start(marks[0:1, par, 0:2 * H * SLOTS], a[f"dst_mark{H}"][bass.ds(g, 1), :]).then_inc(seg_landed[par], 16)
                    if kind == "gat_edge":
                        sp.dma_start(attr[:, par, :], a["attrT"][:, bass.ds(T * P * g, T * P)]).then_inc(seg_landed[par], 16)

                if l == 0:
                    store_tables(sp, -1)
                    group_loop(sp, seg)
                    for s in range(0, min(4, last_stage) + 1):
                        store_tables(sp, s)
                else:
                    group_loop(sp, seg)
                    store_tables(sp, l)

        @block.gpsimd
        def _(pool):
            one_left = Steps(pool, consts)
            one_left.then(nc.gpsimd.memset(ident[:, :], 0.0))
            one_left.then(nc.gpsimd.affine_select(out=ident[:, :], in_=ident[:, :], compare_op=ALU.not_equal, fill=1.0,
                                                  base=0, pattern=[[-1, P]], channel_multiplier=1))
            one_left.then(nc.gpsimd.iota(iota[:, :], pattern=[[1, T * P]], base=0, channel_multiplier=0,
                                         allow_small_or_imprecise_dtypes=True))

            def band(x, pattern, base, mult, width, base2=None):
                one_left.then(nc.gpsimd.memset(x, 1.0))
                one_left.then(nc.gpsimd.affine_select(out=x, in_=x, compare_op=ALU.is_ge, fill=0.0,
                                                      base=base, pattern=pattern, channel_multiplier=mult))
                one_left.then(nc.gpsimd.affine_select(out=x, in_=x, compare_op=ALU.is_ge, fill=0.0, base=width - 1 - base,
                                                      pattern=[[-s, n] for s, n in pattern], channel_multiplier=-mult))

            for H in (8, 4):
                band(head_of[H][:, :, :], [[P, FC], [1, P]], 0, -(D // H), D // H)
                band(head_col[H][:, :, :], [[P, FC], [-(D // H), H]], 0, 1, D // H)
            band(deg_row[:, :], [[0, P]], -8, 1, 1)
            assert one_left.k == CONSTS
            pool.sem_inc(rows_free, 2)
            pool.sem_inc(drows_free, 2)
            pool.sem_inc(seg_free, 2)
            pool.sem_inc(enc_free, 2)
            pool.sem_inc(tb_free, 1)
            pool.wait_ge(loaded, LOADED)
            ring = Steps(pool, pool_step)
            for l in range(n_edge_layers):
                kind = LAYERS[l][0]
                pool.wait_ge(table_written, TABLE_SEM[l + 1])

                def gather(g, h, par, _first, l=l, kind=kind):
                    if kind != "sum":
                        wait_alone(pool, drows_free, 2 * g + 1 if kind == "gat_edge" else DST_BEFORE[l] + g + 1)
                        at = ring.done(nc.gpsimd.tensor_copy(dst_now[:, par, 0:T], dst_idx[:, bass.ds(g * T, T)]))
                        wait_alone(pool, pool_step, at)
                        for k in range(T):
                            if kind == "gat_edge":
                                if k == 4:
                                    wait_alone(pool, drows_free, 2 * g + 2)
                                pool.indirect_dma_start(
                                    drows[:, k // 4, k % 4, :], None, tables[l][:, :],
                                    bass.IndirectOffsetOnAxis(ap=dst_now[:, par, k:k + 1], axis=0)).then_inc(dst_landed[k // 4], 16)
                            else:
                                pool.indirect_dma_start(
                                    dsmall[:, par, k, :], None, scores[l][:, :],
                                    bass.IndirectOffsetOnAxis(ap=dst_now[:, par, k:k + 1], axis=0)).then_inc(dst_landed[par], 16)
                    pool.wait_ge(rows_free, NG * l + g + 1)
                    at = ring.done(nc.gpsimd.tensor_copy(src_now[:, par, 0:T], src_idx[:, bass.ds(g * T, T)]))
                    wait_alone(pool, pool_step, at)
                    for k in range(T):
                        pool.indirect_dma_start(
                            src_rows(l, par)[:, k, :], None, tables[l][:, :],
                            bass.IndirectOffsetOnAxis(ap=src_now[:, par, k:k + 1], axis=0)).then_inc(src_landed[par], 16)

                group_loop(pool, gather, per=2 if kind != "sum" else 1, chain=ring)

        @block.tensor
        def _(pe):
            mm = nc.tensor.matmul
            pe.wait_ge(loaded, LOADED)
            pe.wait_ge(consts, CONSTS)
            pe.wait_ge(built, 1)
            for n, (s, cols) in enumerate(((0, 16), (5, 8), (6, 8))):
                for m in range(FC):
                    for k in range(FC):
                        ins = mm(ps[:, 3 * m + n, 0:cols], part[n][:, k, m * P:(m + 1) * P],
                                 st[:, k, n * 16:n * 16 + cols], start=k == 0, stop=k == 1)
            ins.then_inc(built_pe, 1)
            pe.wait_ge(built, 2)
            turns = Turns(pe, "pe_turns")
            node_pe(pe, -1)
            for l in range(n_edge_layers):
                edge_pe(pe, l, turns)
                node_pe(pe, l)

        @block.scalar
        def _(act):
            act.wait_ge(loaded, LOADED)
            act.wait_ge(built, 2)
            ch = Steps(act, act_step)
            node_act(act, -1)
            for l in range(n_edge_layers):
                if LAYERS[l][0] != "sum":
                    edge_act(act, l, ch)
                node_act(act, l)

        @block.vector
        def _(dve):
            V = nc.vector
            ch = Steps(dve, dve_step)
            dve.sem_inc(added, 1)
            V.memset(mean_w[:, :], 1.0 / D)
            V.memset(eps[:, :], EPS)
            V.memset(unit[:, :], 1.0)
            V.memset(one[:, :], 1.0)
            V.memset(ex8[:, :, :, 8:9], 1.0)
            V.memset(den[:, :], 0.0)
            V.memset(acc[:, :, :], 0.0)
            V.memset(st[:, :, 0:48], 0.0)
            dve.wait_ge(loaded, LOADED)
            dve.wait_ge(consts, CONSTS)
            V.tensor_scalar(floor[:, :], deg_row[:, 0:1], 1e-10, None, ALU.max)
            by_group = lambda x: x[:, :].rearrange("p (g t) -> p g t", t=T)
            V.tensor_tensor(by_group(local), by_group(dst_idx), base[:, :].unsqueeze(2).broadcast_to([P, NG, T]), ALU.subtract)
            ch.then(V.tensor_tensor(windows[:, :], last[:, :], base[0:1, :], ALU.subtract))
            ch.then(V.tensor_scalar(windows[:, :], windows[:, :], 7, None, ALU.arith_shift_right))
            ch.then(V.tensor_scalar(windows[:, :], windows[:, :], 1.0, None, ALU.add))
            for n, H in enumerate((8, 4, 4)):
                for j in range(2):
                    for k in range(FC):
                        ins = V.tensor_scalar(st[:, k, 16 * n + j * H:16 * n + (j + 1) * H], head_col[H][:, k, :],
                                              part[n][:, 0, D + 2 * j + k:D + 2 * j + k + 1], None, ALU.mult)
            ins.then_inc(built, 1)
            dve.wait_ge(built_pe, 1)
            for n, (s, cols) in enumerate(((0, 16), (5, 8), (6, 8))):
                for m in range(FC):
                    ins = V.tensor_copy(w_table[s][:, m, D:D + cols], ps[:, 3 * m + n, 0:cols])
            ins.then_inc(built, 1)
            turns = Turns(dve, "dve_turns")
            ch.flat()
            for l in range(n_edge_layers):
                dve.wait_ge(row_out, 5 * NCH * (l + 1))
                edge_dve(dve, l, ch, turns)
                node_dve(dve, l, ch)


CHAIN_STEPS = {"gat_edge": 16, "gat": 8}
NODE_STEPS = {0: 3, 1: 1, 2: 1, 3: 5, 4: 1, 5: 3, 6: 5}

INS = (["xT", "src_idx", "dst_idx", "base_row", "biases", "w_edge", "attrT"] + [f"w_table{s}" for s in range(NL)]
       + ["w_root1", "w_root2", "w_root3"] + [f"{n}{s}" for s in (0, 5, 6) for n in ("w_out", "score_cols")]
       + ["dst_seg8", "dst_seg4", "dst_mark8", "dst_mark4", "last_row"])


def lay_out(x, src, dst, edge_attr_3, **w):
    import numpy as np
    x, src, dst = np.asarray(x), np.asarray(src), np.asarray(dst)
    o = {}
    o["xT"] = np.zeros((D, NPAD), x.dtype)
    o["xT"][:, :N] = x.T
    dst_p = np.concatenate([np.full(1, -1, dst.dtype), dst, np.full(PAD_E - E + 1, N, dst.dtype)])
    src_p = np.concatenate([src, np.zeros(PAD_E - E, src.dtype)])
    o["src_idx"] = src_p.reshape(TILES, P).T
    o["dst_idx"] = dst_p[1:-1].reshape(TILES, P).T
    o["base_row"] = dst_p[1:-1:T * P]
    o["last_row"] = dst_p[T * P::T * P][None]
    seg = np.stack([dst_p[t * P:t * P + P + 2] for t in range(TILES)])
    ends, starts = dst_p[0::P][:TILES + 1], dst_p[1::P][:TILES + 1]
    for H in (8, 4):
        o[f"dst_seg{H}"] = np.repeat(seg, H, axis=0)
        o[f"dst_mark{H}"] = np.stack([np.concatenate([np.tile(m[g * T:g * T + T + 1], H) for m in (ends, starts)])
                                      for g in range(NG)])
    attr = np.asarray(edge_attr_3)
    o["attrT"] = np.zeros((4, PAD_E), attr.dtype)
    o["attrT"][:3, :E] = attr.T
    o["attrT"][3] = 1
    A = {k: np.asarray(z) for k, z in w.items()}
    o["w_edge"] = np.concatenate([A["L0_gnn_edge_W"].T, A["L0_gnn_edge_b"][None]])
    b = [A["L0_gnn_bias"], A["L1_gnn_b1l"], A["L1_gnn_b2l"], A["L1_gnn_b3l"], A["L2_gnn_b"], A["L3_gnn_b0"], A["L3_gnn_b1"]]
    o["biases"] = np.stack(b).reshape(7 * FC, P).T
    names = ["L0_gnn_W", "L1_gnn_W1l", "L1_gnn_W2l", "L1_gnn_W3l", "L2_gnn_W"]
    for s, n in enumerate(names):
        o[f"w_table{s}"] = A[n].T
    for s, n in ((1, "W1r"), (2, "W2r"), (3, "W3r")):
        o[f"w_root{s}"] = A["L1_gnn_" + n].T
    o["w_table5"], o["w_table6"] = A["L3_gnn_W0"], A["L3_gnn_W1"]
    o["w_out0"], o["w_out5"], o["w_out6"] = A["L0_gnn_W"], A["L3_gnn_W0"].T, A["L3_gnn_W1"].T
    for s, p, q in ((0, "L0_gnn_a_src", "L0_gnn_a_dst"), (5, "L3_gnn_al0", "L3_gnn_ar0"), (6, "L3_gnn_al1", "L3_gnn_ar1")):
        o[f"score_cols{s}"] = np.concatenate([A[p].reshape(FC, P), A[q].reshape(FC, P)]).T
    return o


STOP = None


def kernel(**inputs):
    import numpy as np
    import concourse.bacc as bacc
    from concourse.bass_utils import run_bass_kernel_spmd

    nc = bacc.Bacc("TRN2", target_bir_lowering=False, num_devices=1)
    o = lay_out(**inputs)
    arrays, args = {}, {}
    for name in INS:
        arr = np.ascontiguousarray(o[name])
        arrays[f"in_{name}"] = arr
        args[name] = nc.dram_tensor(f"in_{name}", arr.shape, mybir.dt.from_np(arr.dtype), kind="ExternalInput").ap()
    out = nc.dram_tensor("out_x", (NPAD, D), F32, kind="ExternalOutput").ap()
    gnn_program(nc, args, out, STOP)
    r = run_bass_kernel_spmd(nc, [arrays], core_ids=[0])
    return r.results[0]["out_x"][:N]
```
